# Optimizing a Trainium2 kernel written in Bass

```python
import numpy as np
import jax
import jax.numpy as jnp

def _softmax(x, axis=-1):
    return jax.nn.softmax(x, axis=axis)

def _gelu(x):
    return jax.nn.gelu(x, approximate=True)

def _silu(x):
    return jax.nn.silu(x)

def _sigmoid(x):
    return jax.nn.sigmoid(x)

def _layernorm(x, axis=-1, eps=1e-05):
    m = jnp.mean(x, axis=axis, keepdims=True)
    v = jnp.var(x, axis=axis, keepdims=True)
    return (x - m) / jnp.sqrt(v + eps)

def _scatter_add(tgt, idx, src, axis=0):
    return tgt.at[idx].add(src)

def _segment_sum(src, seg, n):
    return jax.ops.segment_sum(src, seg, n)
kernel_name = 'mk_flamingo_gated_d1_seqx_r8_dba243'

def setup_inputs(seed: int=0):
    np.random.seed(seed)
    _w = jnp.asarray

    def _rec_inputs():
        import jax
        import jax.numpy as jnp
        _rk = jax.random.key(seed)
        x = -0.0003929 + 0.9999 * jax.random.normal(jax.random.fold_in(_rk, 1), (4, 256, 256), jnp.float32)
        _lenS = 256 - jax.random.randint(jax.random.fold_in(_rk, 7), (4,), 0, max(1, 256 // 4) + 1, jnp.int32)
        _lenS2 = 256 - jax.random.randint(jax.random.fold_in(_rk, 8), (4,), 0, max(1, 256 // 4) + 1, jnp.int32)
        _ctx_2048P = jax.random.normal(jax.random.fold_in(_rk, 11), (4, 16, 256), jnp.float32)
        _ctx_2048c = jax.random.dirichlet(jax.random.fold_in(_rk, 511), 0.3 * jnp.ones((16,), jnp.float32), (4, 256))
        _ctx_2048t = jnp.einsum('bsk,bkd->bsd', _ctx_2048c, _ctx_2048P)
        _ctx_2048t = _ctx_2048t * jax.lax.rsqrt(jnp.mean(jnp.square(_ctx_2048t)) + 1e-12) * 0.953939
        ctx_2048 = -1.39393e-06 + 0.999914 * (_ctx_2048t + 0.3 * jax.random.normal(jax.random.fold_in(_rk, 611), (4, 256, 256), jnp.float32))
        itok_BxS_0_1023 = jax.random.randint(jax.random.fold_in(_rk, 12), (4, 256), 0, 128, jnp.int32)
        _g = jax.random.normal(jax.random.fold_in(_rk, 9001), (2, 1), jnp.float32)
        _g = jnp.sign(_g) * jnp.maximum(jnp.abs(_g), 1.0) + (_g == 0) * 1.0
        g_xattn = _g[0]
        g_ffn = _g[1]
        return (x, ctx_2048, itok_BxS_0_1023, g_xattn, g_ffn)
    x, ctx_2048, itok_BxS_0_1023, g_xattn, g_ffn = _rec_inputs()

    def _L0_xattn_setup():
        import jax, jax.numpy as jnp
        import numpy as np
        B, Lq, Lk = (2, 512, 128)
        Q_DIM, KV_DIM = (256, 256)
        H, HD = (16, 128)
        KVC, QC, R = (64, 96, 64)
        LOOKBACK = 8
        NEG = -1e+30

        def _rope(x, L):
            half = x.shape[-1] // 2
            inv_freq = 1.0 / 10000.0 ** (jnp.arange(half, dtype=jnp.float32) / half)
            ang = jnp.arange(L, dtype=jnp.float32)[:, None] * inv_freq
            cos, sin = (jnp.cos(ang), jnp.sin(ang))
            x1, x2 = (x[..., :half], x[..., half:])
            return jnp.concatenate([x1 * cos - x2 * sin, x1 * sin + x2 * cos], axis=-1)
        key = jax.random.key(seed)
        ks = jax.random.split(key, 11)

        def w(k, shape, fan_in):
            return jax.random.normal(k, shape, jnp.float32) / np.sqrt(fan_in).astype(np.float32)
        return {'q': jax.random.normal(ks[0], (B, Lq, Q_DIM), jnp.float32), 'kv': jax.random.normal(ks[1], (B, Lk, KV_DIM), jnp.float32), 'seg_id': jnp.sort(jax.random.randint(ks[2], (B, Lq), 0, Lk), axis=-1), 'W_kvc': w(ks[3], (KV_DIM, KVC), KV_DIM), 'W_dq': w(ks[4], (Q_DIM, QC), Q_DIM), 'W_uq': w(ks[5], (QC, H * HD), QC), 'W_qr': w(ks[6], (QC, H * R), QC), 'W_uk': w(ks[7], (KVC, H * HD), KVC), 'W_kr': w(ks[8], (KVC, R), KVC), 'W_uv': w(ks[9], (KVC, H * HD), KVC), 'W_o': w(ks[10], (H * HD, Q_DIM), H * HD)}
    _L0_xattn_all = _L0_xattn_setup()
    _L0_xattn_in = {k: v for k, v in _L0_xattn_all.items() if k in ('W_kvc', 'W_dq', 'W_uq', 'W_qr', 'W_uk', 'W_kr', 'W_uv', 'W_o')}
    del _L0_xattn_all

    def _L0_ffn_setup():
        import jax, jax.numpy as jnp
        import numpy as np
        EPS = 1e-05

        def rms_norm(x):
            return x * jax.lax.rsqrt(jnp.mean(x * x, axis=-1, keepdims=True) + EPS)

        def act_quant(x):
            scale = 127.0 / jnp.clip(jnp.max(jnp.abs(x), axis=-1, keepdims=True), 1e-05)
            q = jnp.clip(jnp.round(x * scale), -128.0, 127.0) / scale
            return x + jax.lax.stop_gradient(q - x)

        def weight_quant(w):
            scale = 1.0 / jnp.clip(jnp.mean(jnp.abs(w)), 1e-05)
            q = jnp.clip(jnp.round(w * scale), -1.0, 1.0) / scale
            return w + jax.lax.stop_gradient(q - w)

        def bitlinear158(x, w, b):
            xq = act_quant(rms_norm(x))
            wq = weight_quant(w)
            return jnp.einsum('bsd,od->bso', xq, wq) + b

        def layer_norm(x, g, b):
            mu = jnp.mean(x, axis=-1, keepdims=True)
            var = jnp.mean((x - mu) ** 2, axis=-1, keepdims=True)
            return (x - mu) * jax.lax.rsqrt(var + EPS) * g + b
        key = jax.random.key(seed)
        ks = jax.random.split(key, 3)
        d, inner = (256, 1024)
        x = jax.random.normal(ks[0], (4, 256, d), dtype=jnp.float32)
        w1 = jax.random.normal(ks[1], (inner, d), dtype=jnp.float32) * 0.02
        b1 = jnp.zeros((inner,), jnp.float32)
        ln_g = jnp.ones((inner,), jnp.float32)
        ln_b = jnp.zeros((inner,), jnp.float32)
        w2 = jax.random.normal(ks[2], (d, inner), dtype=jnp.float32) * 0.02
        b2 = jnp.zeros((d,), jnp.float32)
        return {'x': x, 'w1': w1, 'b1': b1, 'ln_g': ln_g, 'ln_b': ln_b, 'w2': w2, 'b2': b2}
    _L0_ffn_all = _L0_ffn_setup()
    _L0_ffn_in = {k: v for k, v in _L0_ffn_all.items() if k in ('w1', 'b1', 'ln_g', 'ln_b', 'w2', 'b2')}
    del _L0_ffn_all
    return {'x': x, 'ctx_2048': ctx_2048, 'itok_BxS_0_1023': itok_BxS_0_1023, 'g_xattn': g_xattn, 'g_ffn': g_ffn, 'L0_xattn_W_kvc': _L0_xattn_in['W_kvc'], 'L0_xattn_W_dq': _L0_xattn_in['W_dq'], 'L0_xattn_W_uq': _L0_xattn_in['W_uq'], 'L0_xattn_W_qr': _L0_xattn_in['W_qr'], 'L0_xattn_W_uk': _L0_xattn_in['W_uk'], 'L0_xattn_W_kr': _L0_xattn_in['W_kr'], 'L0_xattn_W_uv': _L0_xattn_in['W_uv'], 'L0_xattn_W_o': _L0_xattn_in['W_o'], 'L0_ffn_w1': _L0_ffn_in['w1'], 'L0_ffn_b1': _L0_ffn_in['b1'], 'L0_ffn_ln_g': _L0_ffn_in['ln_g'], 'L0_ffn_ln_b': _L0_ffn_in['ln_b'], 'L0_ffn_w2': _L0_ffn_in['w2'], 'L0_ffn_b2': _L0_ffn_in['b2']}

def reference(x, ctx_2048, itok_BxS_0_1023, g_xattn, g_ffn, L0_xattn_W_kvc, L0_xattn_W_dq, L0_xattn_W_uq, L0_xattn_W_qr, L0_xattn_W_uk, L0_xattn_W_kr, L0_xattn_W_uv, L0_xattn_W_o, L0_ffn_w1, L0_ffn_b1, L0_ffn_ln_g, L0_ffn_ln_b, L0_ffn_w2, L0_ffn_b2):
    import jax
    import jax.numpy as jnp

    def _L0_xattn_ref(q, kv, seg_id, W_kvc, W_dq, W_uq, W_qr, W_uk, W_kr, W_uv, W_o):
        import jax, jax.numpy as jnp
        import numpy as np
        B, Lq, Lk = (2, 512, 128)
        Q_DIM, KV_DIM = (256, 256)
        H, HD = (16, 128)
        KVC, QC, R = (64, 96, 64)
        LOOKBACK = 8
        NEG = -1e+30

        def _rope(x, L):
            half = x.shape[-1] // 2
            inv_freq = 1.0 / 10000.0 ** (jnp.arange(half, dtype=jnp.float32) / half)
            ang = jnp.arange(L, dtype=jnp.float32)[:, None] * inv_freq
            cos, sin = (jnp.cos(ang), jnp.sin(ang))
            x1, x2 = (x[..., :half], x[..., half:])
            return jnp.concatenate([x1 * cos - x2 * sin, x1 * sin + x2 * cos], axis=-1)
        b, lq, _ = q.shape
        lk = kv.shape[1]
        kv_c = kv @ W_kvc
        q_c = q @ W_dq
        q_nope = (q_c @ W_uq).reshape(b, lq, H, HD).transpose(0, 2, 1, 3)
        q_rope = (q_c @ W_qr).reshape(b, lq, H, R).transpose(0, 2, 1, 3)
        k_nope = (kv_c @ W_uk).reshape(b, lk, H, HD)
        v = (kv_c @ W_uv).reshape(b, lk, H, HD)
        k_rope = kv_c @ W_kr
        q_rope = _rope(q_rope, lq)
        k_rope = _rope(k_rope, lk)
        scale = 1.0 / np.sqrt(HD + R).astype(np.float32)
        scores = (jnp.einsum('bhqd,bkhd->bhqk', q_nope, k_nope) + jnp.einsum('bhqr,bkr->bhqk', q_rope, k_rope)) * scale
        k_ids = jnp.arange(lk)[None, None, :]
        qs = seg_id[:, :, None]
        good = (k_ids <= qs) & (k_ids >= qs - LOOKBACK)
        scores = jnp.where(good[:, None, :, :], scores, NEG)
        attn = jax.nn.softmax(scores, axis=-1)
        out = jnp.einsum('bhqk,bkhd->bqhd', attn, v).reshape(b, lq, H * HD)
        return out @ W_o

    def _L0_ffn_ref(x, w1, b1, ln_g, ln_b, w2, b2):
        import jax, jax.numpy as jnp
        import numpy as np
        EPS = 1e-05

        def rms_norm(x):
            return x * jax.lax.rsqrt(jnp.mean(x * x, axis=-1, keepdims=True) + EPS)

        def act_quant(x):
            scale = 127.0 / jnp.clip(jnp.max(jnp.abs(x), axis=-1, keepdims=True), 1e-05)
            q = jnp.clip(jnp.round(x * scale), -128.0, 127.0) / scale
            return x + jax.lax.stop_gradient(q - x)

        def weight_quant(w):
            scale = 1.0 / jnp.clip(jnp.mean(jnp.abs(w)), 1e-05)
            q = jnp.clip(jnp.round(w * scale), -1.0, 1.0) / scale
            return w + jax.lax.stop_gradient(q - w)

        def bitlinear158(x, w, b):
            xq = act_quant(rms_norm(x))
            wq = weight_quant(w)
            return jnp.einsum('bsd,od->bso', xq, wq) + b

        def layer_norm(x, g, b):
            mu = jnp.mean(x, axis=-1, keepdims=True)
            var = jnp.mean((x - mu) ** 2, axis=-1, keepdims=True)
            return (x - mu) * jax.lax.rsqrt(var + EPS) * g + b
        h = jax.nn.silu(bitlinear158(x, w1, b1))
        h = jax.nn.gelu(h, approximate=False)
        h = layer_norm(h, ln_g, ln_b)
        return bitlinear158(h, w2, b2)
    x = x + jnp.tanh(g_xattn[0]) * _L0_xattn_ref(_layernorm(x, axis=-1), ctx_2048, itok_BxS_0_1023, L0_xattn_W_kvc, L0_xattn_W_dq, L0_xattn_W_uq, L0_xattn_W_qr, L0_xattn_W_uk, L0_xattn_W_kr, L0_xattn_W_uv, L0_xattn_W_o)
    x = x + jnp.tanh(g_ffn[0]) * _L0_ffn_ref(_layernorm(x, axis=-1), L0_ffn_w1, L0_ffn_b1, L0_ffn_ln_g, L0_ffn_ln_b, L0_ffn_w2, L0_ffn_b2)
    return x

_drawn_inputs = setup_inputs


def setup_inputs(seed=0):
    import zlib

    import numpy as np

    out = dict(_drawn_inputs(seed))
    spreads = {'L0_ffn_b1': (0.0, 0.1),
     'L0_ffn_ln_g': (1.0, 0.2),
     'L0_ffn_ln_b': (0.0, 0.1),
     'L0_ffn_b2': (0.0, 0.1)}
    factors = {}
    for name, (base, spread) in spreads.items():
        noise = np.random.default_rng([zlib.crc32(name.encode()), seed]).standard_normal(out[name].shape)
        drawn = base * np.exp(spread * noise) if base else spread * noise
        out[name] = jnp.asarray(drawn.astype(out[name].dtype))
    for name, factor in factors.items():
        out[name] = (out[name] * factor).astype(out[name].dtype)
    return out
```

```python
from contextlib import ExitStack

import numpy as np
import concourse.bass as bass
from concourse import mybir

B, S, D = 4, 256, 256
H, HD, R = 16, 128, 64
KVC, QC = 64, 96
INNER = 1024
LOOKBACK = 8
P = 128
TILES = S // P
DC = D // P
IC = INNER // P
PAIRS = H // 2
GROUP = 4
STEPS = TILES * H // GROUP
AHEAD = STEPS - 2
SCALE = float(1.0 / np.sqrt(np.float32(HD + R)))
NEG = -1e30
EPS = 1e-5
MAGIC = 12582912.0
QMAX = 127.0
EYE, IOTA, COS, SIN, CONSTS = 0, P, P + S, P + 3 * S, P + 4 * S


def shape_constants():
    half = R // 2
    freq = (np.float32(1.0) / np.float32(10000.0) ** (np.arange(half, dtype=np.float32) / np.float32(half)))
    ang = np.arange(S, dtype=np.float32)[None, :] * freq.astype(np.float32)[:, None]
    cos, sin = np.cos(ang).astype(np.float32), np.sin(ang).astype(np.float32)
    one = np.ones((KVC, S), np.float32)
    c = np.zeros((P, CONSTS), np.float32)
    c[:, EYE:EYE + P] = np.eye(P, dtype=np.float32)
    c[:, IOTA:IOTA + S] = np.arange(S, dtype=np.float32)[None, :] + LOOKBACK / 2
    c[:, COS:COS + S] = np.concatenate([one, cos, cos])
    c[:, COS + S:COS + 2 * S] = np.concatenate([cos, cos, one])
    c[:, SIN:SIN + S] = np.concatenate([-sin, sin, -sin, sin])
    return c


def build(nc, x, ctx_kv, itok, g_xattn, g_ffn, W_kvc, W_dq, W_uq, W_qr, W_uk, W_kr, W_uv, W_o,
          w1, b1, ln_g, ln_b, w2, b2, consts, out):
    fp32, bf16, i32 = mybir.dt.float32, mybir.dt.bfloat16, mybir.dt.int32
    ALU, ACT, AX = mybir.AluOpType, mybir.ActivationFunctionType, mybir.AxisListType
    KT = S // P

    with ExitStack() as stack:
        def sb(name, shape, dt=fp32):
            return stack.enter_context(nc.sbuf_tensor(name, shape, dt))

        def ps(name, shape, dt=fp32):
            return stack.enter_context(nc.psum_tensor(name, shape, dt))

        def sem(name):
            return stack.enter_context(nc.semaphore(name))

        x_all = sb("x_all", [P, B * TILES, D])
        ctx_all = sb("ctx_all", [P, B * TILES, D])
        seg_i = sb("seg_i", [P, B * TILES], i32)
        cst = sb("cst", [P, CONSTS])
        wdq = sb("wdq", [P, DC, QC])
        wkvc = sb("wkvc", [P, DC, KVC])
        wkr = sb("wkr", [KVC, R])
        wuq_room = sb("wuq_room", [P, H * HD])
        wuk_room = sb("wuk_room", [P, H * HD])
        wuv_room = sb("wuv_room", [P, H * HD])
        wuq = wuq_room[0:QC, :].rearrange("k (h n) -> k h n", h=H)
        wqr = sb("wqr", [QC, H, R])
        wuk = wuk_room[0:KVC, :].rearrange("k (h n) -> k h n", h=H)
        wuv = wuv_room[0:KVC, :].rearrange("k (h n) -> k h n", h=H)
        wo = sb("wo", [HD, H, D])
        w1_sb = sb("w1_sb", [P, IC, D])
        w2_sb = sb("w2_sb", [P, DC, INNER])
        b1_bc = sb("b1_bc", [P, INNER])
        g_bc = sb("g_bc", [P, INNER])
        lb_bc = sb("lb_bc", [P, INNER])
        b2_bc = sb("b2_bc", [P, D])
        gates = sb("gates", [P, 2])

        prep_room = sb("prep_room", [P, H * (QC + 2 * KVC)])
        wuqT = prep_room[:, 0:H * QC].rearrange("p (h c) -> p h c", h=H)
        wukT = prep_room[:, H * QC:H * (QC + KVC)].rearrange("p (h c) -> p h c", h=H)
        wuvT = prep_room[:, H * (QC + KVC):H * (QC + 2 * KVC)].rearrange("p (h c) -> p h c", h=H)
        wcat = sb("wcat", [QC, PAIRS, 2, P])
        wswap = sb("wswap", [QC, PAIRS, P])
        kcat_w = sb("kcat_w", [KVC, 2, P])
        kswap_w = sb("kswap_w", [KVC, P])
        m_sb = sb("m_sb", [P, PAIRS, D])
        w1T = sb("w1T", [P, DC, INNER], bf16)
        w2T = sb("w2T", [P, IC, D], bf16)
        w1q = sb("w1q", [P, IC * D], bf16)
        w2q = sb("w2q", [P, DC * INNER], bf16)

        eye_b = sb("eye_b", [P, P], bf16)
        ones = sb("ones", [P, P])
        half_neg = sb("half_neg", [P, 2])
        mask = sb("mask", [P, B * TILES, S], bf16)
        seg_f = sb("seg_f", [P, B * TILES])
        dist = sb("dist", [P, 2, S])
        tgate = sb("tgate", [P, 2])
        wabs = sb("wabs", [P, 2])
        wmean = sb("wmean", [P, 2])
        winv = sb("winv", [P, 2])

        xn = sb("xn", [P, TILES, D])
        prob_room = sb("prob_room", [P, 2 * GROUP * KT * P])
        xnT = prob_room[:, 0:DC * S].rearrange("p (c s) -> p c s", c=DC)
        ctxT = prob_room[:, DC * S:2 * DC * S].rearrange("p (c s) -> p c s", c=DC)
        qcT = sb("qcT", [QC, B * S])
        kvcT = sb("kvcT", [KVC, S])
        kcat = sb("kcat", [P, B, 2, S])
        kvc1 = sb("kvc1", [P, B * KT, KVC + 1])

        qcat = sb("qcat", [P, PAIRS, 2, S])
        turned = sb("turned", [P, 2, S])
        prob = prob_room[:, :].rearrange("p (n h s) -> p n h s", n=2, h=GROUP)
        probT = wuq_room[:, 0:2 * KT * GROUP * P].rearrange("p (n t h s) -> p n t h s", n=2, t=KT, h=GROUP)
        smax = sb("smax", [P, 2, GROUP])
        rsum = sb("rsum", [P, 2, GROUP])
        lat = sb("lat", [P, 2, GROUP, KVC])
        latT = wuk_room[:, 0:TILES * PAIRS * P].rearrange("p (t j s) -> p t j s", t=TILES, j=PAIRS)

        x1, xl, ytmp, y = (wuv_room[:, i * TILES * D:(i + 1) * TILES * D].rearrange("p (t n) -> p t n", t=TILES)
                           for i in range(4))
        xqT = sb("xqT", [P, TILES, DC, P], bf16)
        h = prep_room[:, 0:TILES * INNER].rearrange("p (t n) -> p t n", t=TILES)
        hqT = sb("hqT", [P, TILES, IC, P], bf16)
        junk = prep_room[:, TILES * INNER:(TILES + 1) * INNER].bitcast(bf16).rearrange("p (t n) -> p t n", t=TILES)
        stats = sb("stats", [P, TILES, 12])
        mv = sb("mv", [P, TILES, 2])
        var = sb("var", [P, TILES])
        rstd = sb("rstd", [P, TILES])
        amax = sb("amax", [P, TILES])
        sumsq = sb("sumsq", [P, TILES])
        msq = sb("msq", [P, TILES])
        rrms = sb("rrms", [P, TILES])
        ymax = sb("ymax", [P, TILES])
        yinv = sb("yinv", [P, TILES])
        qmul = sb("qmul", [P, TILES])
        deq = sb("deq", [P, 2, TILES])

        bank_pair = ps("bank_pair", [P, 512])
        bank_swap = ps("bank_swap", [P, 512])
        bank_score = ps("bank_score", [P, 2, 512])
        bank_prob = ps("bank_prob", [P, 512])
        bank_lat = ps("bank_lat", [P, 512])
        bank_ff = ps("bank_ff", [P, TILES, 512])

        in_sems = {n: sem("in_" + n) for n in (
            "x", "ctx", "seg", "cst", "wdq", "wkvc", "wkr", "wuq", "wqr", "wuk", "wuv", "wo", "w1", "w2",
            "b1", "g", "lb", "b2", "gate0", "gate1")}
        out_stored = sem("out_stored")
        consts_made = sem("consts_made")
        mask_made = sem("mask_made")
        kweights = sem("kweights")
        wcopies = sem("wcopies")
        gates_done = sem("gates_done")
        a_var = sem("a_var")
        a_rstd = sem("a_rstd")
        xn_ready = sem("xn_ready")
        xT_ready = sem("xT_ready")
        xT_copied = sem("xT_copied")
        cT_ready = sem("cT_ready")
        cT_copied = sem("cT_copied")
        qc_ready = sem("qc_ready")
        qc_copied = sem("qc_copied")
        kvc_ready = sem("kvc_ready")
        kvc_copied = sem("kvc_copied")
        kvk_ready = sem("kvk_ready")
        kvk_copied = sem("kvk_copied")
        wt_ready = sem("wt_ready")
        wt_copied = sem("wt_copied")
        fold_ready = sem("fold_ready")
        fold_copied = sem("fold_copied")
        m_ready = sem("m_ready")
        m_copied = sem("m_copied")
        wabs_ready = sem("wabs_ready")
        wtot_ready = sem("wtot_ready")
        wq_ready = sem("wq_ready")
        wqT_ready = sem("wqT_ready")
        wqT_copied = sem("wqT_copied")
        pair_ready = sem("pair_ready")
        pair_turned = sem("pair_turned")
        pair_half = sem("pair_half")
        pair_done = sem("pair_done")
        score_ready = sem("score_ready")
        smax_done = sem("smax_done")
        shifted = sem("shifted")
        exp_done = sem("exp_done")
        probT_ready = sem("probT_ready")
        probT_copied = sem("probT_copied")
        lat_ready = sem("lat_ready")
        rsum_done = sem("rsum_done")
        lat_done = sem("lat_done")
        latT_ready = sem("latT_ready")
        latT_copied = sem("latT_copied")
        attn_ready = sem("attn_ready")
        x_var = sem("x_var")
        x_rstd = sem("x_rstd")
        xl_ready = sem("xl_ready")
        x_sumsq = sem("x_sumsq")
        x_ms = sem("x_ms")
        x_rrms = sem("x_rrms")
        xq_ready = sem("xq_ready")
        xqT_ready = sem("xqT_ready")
        xqT_copied = sem("xqT_copied")
        up_ready = sem("up_ready")
        z_done = sem("z_done")
        silu_done = sem("silu_done")
        gelu_done = sem("gelu_done")
        h_var = sem("h_var")
        h_rstd = sem("h_rstd")
        h_norm = sem("h_norm")
        h_scaled = sem("h_scaled")
        h_ready0 = sem("h_ready0")
        h_ready1 = sem("h_ready1")
        h_sumsq = sem("h_sumsq")
        h_ms = sem("h_ms")
        h_rrms = sem("h_rrms")
        hq_ready = sem("hq_ready")
        hqT_ready = sem("hqT_ready")
        hqT_copied = sem("hqT_copied")
        down_ready = sem("down_ready")
        y_done = sem("y_done")
        dve_link = sem("dve_link")

        eye = cst[:, EYE:EYE + P]
        iota = cst[:, IOTA:IOTA + S]
        cos_tab = cst[:, COS:COS + 2 * S].rearrange("p (e s) -> p e s", e=2)
        sin_tab = cst[:, SIN:SIN + S]

        def back(b, k, d):
            return (b, k - d) if k >= d else (b - 1, k - d + STEPS)

        def step_no(b, k):
            return b * STEPS + k

        def pair_at(b, k):
            bb, j = (b + 1, k - 2) if k >= 2 else (b, k + AHEAD)
            return bb, j, B + bb * PAIRS + j

        def pair_in_step(b, k, last):
            return not (last and k >= 2)

        def run_batches(eng, body):
            body(0, True, False)
            with eng.Fori(1, B - 1) as b:
                body(b, False, False)
            body(B - 1, False, True)

        block = stack.enter_context(nc.Block())

        @block.sync
        def _(sp):
            def load(dst, src, name):
                sp.dma_start(dst, src).then_inc(in_sems[name], 16)

            load(cst[:, :], consts, "cst")
            load(x_all[:, :, :], x.rearrange("b (t p) d -> p (b t) d", p=P), "x")
            load(wdq[:, :, :], W_dq.rearrange("(c p) n -> p c n", p=P), "wdq")
            load(wuq, W_uq.rearrange("k (h n) -> k h n", h=H), "wuq")
            load(wuk, W_uk.rearrange("k (h n) -> k h n", h=H), "wuk")
            load(wo[:, :, :], W_o.rearrange("(h p) n -> p h n", p=P), "wo")
            load(w2_sb[:, :, :], w2.rearrange("(c p) n -> p c n", p=P), "w2")
            load(g_bc[:, :], ln_g.partition_broadcast(P), "g")
            load(lb_bc[:, :], ln_b.partition_broadcast(P), "lb")

            def body(b, first, last):
                if first:
                    return
                store(b - 1)

            def store(c):
                sp.wait_ge(y_done, c + 1)
                sp.dma_start(out[bass.ds(c, 1), :, :].rearrange("o (t p) d -> p (o t) d", p=P),
                             y[:, :, :]).then_inc(out_stored, 16)

            run_batches(sp, body)
            store(B - 1)
            sp.wait_ge(out_stored, 16 * B)

        @block.gpsimd
        def _(pool):
            pool.wait_ge(in_sems["cst"], 16)
            pool.wait_ge(in_sems["wkr"], 16)
            half = R // 2
            nc.gpsimd.tensor_copy(kcat_w[:, 0, 0:KVC], eye[0:KVC, 0:KVC])
            nc.gpsimd.tensor_copy(kcat_w[:, 0, KVC:P], wkr[:, :])
            nc.gpsimd.tensor_copy(kcat_w[:, 1, 0:R], wkr[:, :])
            nc.gpsimd.tensor_copy(kcat_w[:, 1, R:P], eye[0:KVC, 0:KVC])
            for o in (0, R):
                nc.gpsimd.tensor_copy(kswap_w[:, o:o + half], wkr[:, half:R])
                last = nc.gpsimd.tensor_copy(kswap_w[:, o + half:o + R], wkr[:, 0:half])
            last.then_inc(kweights, 1)
            pool.wait_ge(in_sems["wqr"], 16)
            wqr_pair = wqr[:, :, :].rearrange("k (j e) n -> k j e n", e=2)
            nc.gpsimd.tensor_copy(wcat[:, :, 0, KVC:P], wqr_pair[:, :, 0, :])
            nc.gpsimd.tensor_copy(wcat[:, :, 1, 0:R], wqr_pair[:, :, 1, :])
            for o, e in ((0, 1), (R, 0)):
                nc.gpsimd.tensor_copy(wswap[:, :, o:o + half], wqr_pair[:, :, e, half:R])
                last = nc.gpsimd.tensor_copy(wswap[:, :, o + half:o + R], wqr_pair[:, :, e, 0:half])
            last.then_inc(wcopies, 1)

            def rsqrt(dst, src, ready, done, n):
                pool.wait_ge(ready, n)
                nc.gpsimd.tensor_tensor(dst, src, half_neg[:, :], ALU.pow).then_inc(done, 1)

            def add_rope(dst, s, slot):
                pool.wait_ge(pair_turned, s + 1)
                nc.gpsimd.tensor_tensor(dst[0:R, 1, :], dst[0:R, 1, :], turned[0:R, slot, :], ALU.add).then_inc(pair_half, 1)
                pool.wait_ge(pair_half, s + 1)
                nc.gpsimd.tensor_tensor(dst[KVC:P, 0, :], dst[KVC:P, 0, :], turned[KVC:P, slot, :], ALU.add).then_inc(pair_done, 1)
                pool.wait_ge(pair_done, s + 1)

            pool.wait_ge(consts_made, 1)
            with pool.Fori(0, B) as b:
                rsqrt(rstd[:, :], var[:, :], a_var, a_rstd, b + 1)
                add_rope(kcat[:, b, :, :], b, 0)

            for j in range(AHEAD):
                add_rope(qcat[:, j, :, :], B + j, j % 2)

            def feed_forward(c, k):
                if k == 2:
                    rsqrt(rstd[:, :], var[:, :], x_var, x_rstd, c + 1)
                    rsqrt(rrms[:, :], msq[:, :], x_ms, x_rrms, c + 1)
                if k == 5:
                    rsqrt(rstd[:, :], var[:, :], h_var, h_rstd, c + 1)
                if k == 6:
                    pool.wait_ge(h_norm, c + 1)
                    nc.gpsimd.tensor_tensor(h[:, 1, :], h[:, 1, :], g_bc[:, :], ALU.mult).then_inc(h_scaled, 1)
                    pool.wait_ge(h_scaled, c + 1)
                    nc.gpsimd.tensor_tensor(h[:, 1, :], h[:, 1, :], lb_bc[:, :], ALU.add).then_inc(h_ready1, 1)
                    rsqrt(rrms[:, :], msq[:, :], h_ms, h_rrms, c + 1)

            pool.wait_ge(in_sems["g"], 16)
            pool.wait_ge(in_sems["lb"], 16)

            def body(b, first, last):
                for k in range(STEPS):
                    if pair_in_step(b, k, last):
                        bb, j, s = pair_at(b, k)
                        add_rope(qcat[:, j, :, :], s, j % 2)
                    if not first:
                        feed_forward(b - 1, k)

            run_batches(pool, body)
            for k in range(STEPS):
                feed_forward(B - 1, k)

        @block.scalar
        def _(act):
            def load(dst, src, name):
                act.dma_start(dst, src).then_inc(in_sems[name], 16)

            load(ctx_all[:, :, :], ctx_kv.rearrange("b (t p) d -> p (b t) d", p=P), "ctx")
            load(wkvc[:, :, :], W_kvc.rearrange("(c p) n -> p c n", p=P), "wkvc")
            load(wkr[:, :], W_kr, "wkr")
            load(wqr[:, :, :], W_qr.rearrange("k (h n) -> k h n", h=H), "wqr")
            load(gates[:, 0:1], g_xattn.partition_broadcast(P), "gate0")
            load(gates[:, 1:2], g_ffn.partition_broadcast(P), "gate1")
            with nc.allow_non_contiguous_dma(reason="1024 token numbers"):
                load(seg_i[:, :], itok.rearrange("b (t p) -> p (b t)", p=P), "seg")
            load(wuv, W_uv.rearrange("k (h n) -> k h n", h=H), "wuv")
            load(w1_sb[:, :, :], w1.rearrange("(c p) n -> p c n", p=P), "w1")
            load(b1_bc[:, :], b1.partition_broadcast(P), "b1")
            load(b2_bc[:, :], b2.partition_broadcast(P), "b2")

            act.wait_ge(in_sems["gate0"], 16)
            act.wait_ge(in_sems["gate1"], 16)
            nc.scalar.activation(tgate[:, :], gates[:, :], ACT.Tanh).then_inc(gates_done, 1)

            with act.Fori(0, B) as b:
                act.wait_ge(xT_ready, b + 1)
                nc.scalar.copy(xnT[:, :, :], bank_score[:, 0, :].rearrange("p (c s) -> p c s", c=DC)).then_inc(xT_copied, 1)
                act.wait_ge(kvc_ready, b + 1)
                nc.scalar.copy(kvcT[:, :], bank_lat[0:KVC, 0:S]).then_inc(kvc_copied, 1)
                act.wait_ge(qc_ready, b + 1)
                nc.scalar.copy(qcT[:, bass.ds(b * S, S)], bank_prob[0:QC, 0:S]).then_inc(qc_copied, 1)
                act.wait_ge(kvk_ready, b + 1)
                act.wait_ge(consts_made, 1)
                nc.scalar.copy(kvc1[:, bass.ds(b * KT, KT), 0:KVC],
                               bank_ff[:, 0, 0:KT * KVC].rearrange("p (t c) -> p t c", t=KT)).then_inc(kvk_copied, 1)

            for i in range(H // 4):
                act.wait_ge(wt_ready, i + 1)
                nc.scalar.copy(wuqT[:, 4 * i:4 * i + 4, :],
                               bank_score[:, 0, 0:4 * QC].rearrange("p (h c) -> p h c", h=4))
                nc.scalar.copy(wukT[:, 4 * i:4 * i + 4, :],
                               bank_score[:, 1, 0:4 * KVC].rearrange("p (h c) -> p h c", h=4)).then_inc(wt_copied, 1)
            for i in range(H // 8):
                act.wait_ge(wt_ready, H // 4 + i + 1)
                nc.scalar.copy(wuvT[:, 8 * i:8 * i + 8, :],
                               bank_score[:, i, :].rearrange("p (h c) -> p h c", h=8)).then_inc(wt_copied, 1)
            for i in range(4):
                act.wait_ge(wqT_ready, i + 1)
                src = bank_ff[:, i % 2, :].bitcast(bf16)
                dst = w1T[:, i, :] if i < 2 else w2T[:, 4 * (i - 2):4 * (i - 1), :]
                if i >= 2:
                    src = src.rearrange("p (c n) -> p c n", c=4)
                nc.scalar.copy(dst, src).then_inc(wqT_copied, 1)

            def feed_forward(c, k):
                if k == 2:
                    act.wait_ge(xl_ready, c + 1)
                    for t in range(TILES):
                        last = nc.scalar.activation(junk[:, t, 0:D], xl[:, t, :], ACT.Square, accum_out=sumsq[:, t:t + 1])
                    last.then_inc(x_sumsq, 1)
                    act.wait_ge(xqT_ready, c + 1)
                    for t in range(TILES):
                        last = nc.scalar.activation(xqT[:, t, :, :], bank_ff[:, t, 0:D].rearrange("p (c s) -> p c s", c=DC),
                                                    ACT.Copy, bias=-MAGIC)
                    last.then_inc(xqT_copied, 1)
                if k == 4:
                    act.wait_ge(z_done, 2 * c + 2)
                    nc.scalar.activation(h[:, :, :], h[:, :, :], ACT.Silu).then_inc(silu_done, 1)
                    act.wait_ge(silu_done, c + 1)
                    nc.scalar.activation(h[:, :, :], h[:, :, :], ACT.Gelu).then_inc(gelu_done, 1)
                if k == 6:
                    act.wait_ge(h_ready0, c + 1)
                    nc.scalar.activation(junk[:, 0, :], h[:, 0, :], ACT.Square, accum_out=sumsq[:, 0:1])
                    act.wait_ge(h_ready1, c + 1)
                    nc.scalar.activation(junk[:, 1, :], h[:, 1, :], ACT.Square, accum_out=sumsq[:, 1:2]).then_inc(h_sumsq, 1)
                if k == 7:
                    for r in range(2):
                        act.wait_ge(hqT_ready, 2 * c + r + 1)
                        for t in range(TILES):
                            last = nc.scalar.activation(hqT[:, t, 4 * r:4 * r + 4, :],
                                                        bank_ff[:, t, :].rearrange("p (c s) -> p c s", c=4),
                                                        ACT.Copy, bias=-MAGIC)
                        last.then_inc(hqT_copied, 1)

            def copy_latT(b, k):
                n = step_no(b, k)
                g, t = k // 2, k % 2
                act.wait_ge(latT_ready, n + 1)
                if not (isinstance(b, int) and b == 0):
                    act.wait_ge(attn_ready, b)
                nc.scalar.copy(latT[:, t, 2 * g:2 * g + 2, :],
                               bank_lat[:, 0:2 * P].rearrange("p (j s) -> p j s", j=2)).then_inc(latT_copied, 1)

            def copy_probT(b, k):
                n = step_no(b, k)
                if not (isinstance(b, int) and n < 2):
                    act.wait_ge(lat_ready, n - 1)
                for kt in range(KT):
                    act.wait_ge(probT_ready, n * KT + kt + 1)
                    nc.scalar.copy(probT[:, k % 2, kt, :, :],
                                   bank_prob[:, :].rearrange("p (h s) -> p h s", h=GROUP)).then_inc(probT_copied, 1)

            def body(b, first, last):
                for k in range(STEPS):
                    n = step_no(b, k)
                    if not (first and k < 2):
                        copy_latT(*back(b, k, 2))
                    if not (first and k < 1):
                        copy_probT(*back(b, k, 1))
                    act.wait_ge(shifted, n + 1)
                    nc.scalar.activation(prob[:, k % 2, :, :], prob[:, k % 2, :, :], ACT.Exp, scale=SCALE).then_inc(exp_done, 1)
                    if not first:
                        feed_forward(b - 1, k)

            run_batches(act, body)
            copy_latT(B - 1, STEPS - 2)
            copy_probT(B - 1, STEPS - 1)
            copy_latT(B - 1, STEPS - 1)
            for k in range(STEPS):
                feed_forward(B - 1, k)

        @block.tensor
        def _(pe):
            def project_pair(w, ws, src, s):
                if not (isinstance(s, int) and s == 0):
                    pe.wait_ge(pair_turned, s)
                for e in range(2):
                    nc.tensor.matmul(bank_pair[:, e * S:(e + 1) * S], w[:, e, :], src, start=(e == 0), stop=(e == 1), skip_group_check=True)
                nc.tensor.matmul(bank_swap[:, 0:S], ws, src, start=True, stop=True).then_inc(pair_ready, 1)

            pe.wait_ge(in_sems["cst"], 16)
            pe.wait_ge(in_sems["ctx"], 16)
            pe.wait_ge(in_sems["wkvc"], 16)
            pe.wait_ge(in_sems["wdq"], 16)
            pe.wait_ge(kweights, 1)
            for b in range(B):
                if b:
                    pe.wait_ge(cT_copied, b)
                for t in range(TILES):
                    for c in range(DC):
                        last = nc.tensor.transpose(bank_score[:, 1, c * S + t * P:c * S + (t + 1) * P],
                                                   ctx_all[:, b * TILES + t, c * P:(c + 1) * P], eye)
                last.then_inc(cT_ready, 1)
                pe.wait_ge(xn_ready, b + 1)
                if b:
                    pe.wait_ge(xT_copied, b)
                for t in range(TILES):
                    for c in range(DC):
                        last = nc.tensor.transpose(bank_score[:, 0, c * S + t * P:c * S + (t + 1) * P],
                                                   xn[:, t, c * P:(c + 1) * P], eye)
                last.then_inc(xT_ready, 1)
                pe.wait_ge(cT_copied, b + 1)
                if b:
                    pe.wait_ge(kvc_copied, b)
                for c in range(DC):
                    last = nc.tensor.matmul(bank_lat[0:KVC, 0:S], wkvc[:, c, :], ctxT[:, c, :], start=(c == 0), stop=(c == DC - 1))
                last.then_inc(kvc_ready, 1)
                pe.wait_ge(xT_copied, b + 1)
                if b:
                    pe.wait_ge(qc_copied, b)
                for c in range(DC):
                    last = nc.tensor.matmul(bank_prob[0:QC, 0:S], wdq[:, c, :], xnT[:, c, :], start=(c == 0), stop=(c == DC - 1))
                last.then_inc(qc_ready, 1)
                pe.wait_ge(kvc_copied, b + 1)
                project_pair(kcat_w, kswap_w[:, :], kvcT[:, :], b)
                if b:
                    pe.wait_ge(kvk_copied, b)
                for kt in range(KT):
                    last = nc.tensor.transpose(bank_ff[:, 0, kt * KVC:(kt + 1) * KVC], kvcT[:, kt * P:(kt + 1) * P],
                                               eye[0:KVC, 0:KVC])
                last.then_inc(kvk_ready, 1)

            pe.wait_ge(in_sems["wuq"], 16)
            pe.wait_ge(in_sems["wuk"], 16)
            pe.wait_ge(xT_copied, B)
            pe.wait_ge(cT_copied, B)
            pe.wait_ge(qc_copied, B)
            for i in range(H // 4):
                if i:
                    pe.wait_ge(wt_copied, i)
                for j in range(4):
                    nc.tensor.transpose(bank_score[:, 0, j * QC:(j + 1) * QC], wuq[:, 4 * i + j, :], eye[0:QC, 0:QC])
                    last = nc.tensor.transpose(bank_score[:, 1, j * KVC:(j + 1) * KVC], wuk[:, 4 * i + j, :], eye[0:KVC, 0:KVC])
                last.then_inc(wt_ready, 1)
                pe.wait_ge(wt_copied, i + 1)
                if i:
                    pe.wait_ge(fold_copied, i)
                for j in range(4):
                    last = nc.tensor.matmul(bank_prob[0:QC, j * KVC:(j + 1) * KVC], wuqT[:, 4 * i + j, :], wukT[:, 4 * i + j, :],
                                            start=True, stop=True)
                last.then_inc(fold_ready, 1)

            pe.wait_ge(in_sems["wuv"], 16)
            for i in range(H // 8):
                for j in range(8):
                    last = nc.tensor.transpose(bank_score[:, i, j * KVC:(j + 1) * KVC], wuv[:, 8 * i + j, :], eye[0:KVC, 0:KVC])
                last.then_inc(wt_ready, 1)
            pe.wait_ge(in_sems["wo"], 16)
            pe.wait_ge(wt_copied, H // 4 + 2)
            pe.wait_ge(kvk_copied, B)
            for i in range(H // 4):
                if i >= 2:
                    pe.wait_ge(m_copied, i - 1)
                for j in range(4):
                    hh = 4 * i + j
                    last = nc.tensor.matmul(bank_ff[(j % 2) * KVC:(j % 2 + 1) * KVC, i % 2, (j // 2) * D:(j // 2 + 1) * D],
                                            wuvT[:, hh, :], wo[:, hh, :], start=True, stop=True)
                last.then_inc(m_ready, 1)

            pe.wait_ge(wabs_ready, 1)
            pe.wait_ge(kvc_copied, B)
            nc.tensor.matmul(bank_lat[:, 0:2], ones[:, :], wabs[:, :], start=True, stop=True).then_inc(wtot_ready, 1)
            pe.wait_ge(wq_ready, 1)
            pe.wait_ge(m_copied, H // 4)
            for i in range(4):
                if i >= 2:
                    pe.wait_ge(wqT_copied, i - 1)
                dst = bank_ff[:, i % 2, :].bitcast(bf16)
                for j in range(8):
                    if i < 2:
                        src = w1q[:, j * D + i * P:j * D + (i + 1) * P]
                    else:
                        ic, dc = 4 * (i - 2) + j // 2, j % 2
                        src = w2q[:, dc * INNER + ic * P:dc * INNER + (ic + 1) * P]
                    last = nc.tensor.transpose(dst[:, j * P:(j + 1) * P], src, eye_b[:, :])
                last.then_inc(wqT_ready, 1)
            pe.wait_ge(wqT_copied, 4)

            pe.wait_ge(wcopies, 1)
            pe.wait_ge(fold_copied, H // 4)
            for j in range(AHEAD):
                project_pair(wcat[:, j, :, :], wswap[:, j, :], qcT[:, 0:S], B + j)

            def scores(b, k):
                n = step_no(b, k)
                g, t = k // 2, k % 2
                if not (isinstance(b, int) and n == 0):
                    pe.wait_ge(shifted, n)
                pe.wait_ge(pair_done, B + b * PAIRS + 2 * g + 2)
                per = GROUP // KT
                for i in range(KT):
                    nc.tensor.matmul(bank_score[:, i, :].rearrange("p (h s) -> p h s", h=per), eye_b[:, :],
                                     mask[:, bass.ds(b * TILES + t, 1), 0:KT * P].broadcast_to([P, per, KT * P]),
                                     start=True, stop=False, skip_group_check=True)
                    for j in range(per):
                        hh = GROUP * g + per * i + j
                        last = nc.tensor.matmul(bank_score[:, i, j * KT * P:(j + 1) * KT * P],
                                                qcat[:, hh // 2, hh % 2, t * P:(t + 1) * P],
                                                kcat[:, b, hh % 2, 0:KT * P],
                                                start=False, stop=(j == per - 1), skip_group_check=True)
                last.then_inc(score_ready, 1)

            def transpose_probs(b, k):
                n = step_no(b, k)
                pe.wait_ge(exp_done, n + 1)
                for kt in range(KT):
                    if not (isinstance(b, int) and n * KT + kt == 0):
                        pe.wait_ge(probT_copied, n * KT + kt)
                    for j in range(GROUP):
                        last = nc.tensor.transpose(bank_prob[:, j * P:(j + 1) * P], prob[:, k % 2, j, kt * P:(kt + 1) * P], eye)
                    last.then_inc(probT_ready, 1)

            def values(b, k):
                n = step_no(b, k)
                pe.wait_ge(probT_copied, (n + 1) * KT)
                if not (isinstance(b, int) and n == 0):
                    pe.wait_ge(latT_copied, n)
                for j in range(GROUP):
                    for kt in range(KT):
                        last = nc.tensor.matmul(bank_lat[:, j * (KVC + 1):(j + 1) * (KVC + 1)], probT[:, k % 2, kt, j, :],
                                                kvc1[:, b * KT + kt, :], start=(kt == 0), stop=(kt == KT - 1))
                last.then_inc(lat_ready, 1)

            def transpose_lat(b, k):
                n = step_no(b, k)
                pe.wait_ge(lat_done, n + 1)
                for j in range(2):
                    last = nc.tensor.transpose(bank_lat[:, j * P:(j + 1) * P],
                                               lat[:, k % 2, 2 * j:2 * j + 2, :].rearrange("p h c -> p (h c)"), eye)
                last.then_inc(latT_ready, 1)

            def attn_out(c):
                pe.wait_ge(latT_copied, (c + 1) * STEPS)
                if not (isinstance(c, int) and c == 0):
                    pe.wait_ge(y_done, c)
                for t in range(TILES):
                    for j in range(PAIRS):
                        last = nc.tensor.matmul(bank_ff[:, t, 0:D], latT[:, t, j, :], m_sb[:, j, :],
                                                start=(j == 0), stop=(j == PAIRS - 1))
                last.then_inc(attn_ready, 1)

            def transpose_x(c):
                pe.wait_ge(xq_ready, c + 1)
                for t in range(TILES):
                    for j in range(DC):
                        last = nc.tensor.transpose(bank_ff[:, t, j * P:(j + 1) * P], xl[:, t, j * P:(j + 1) * P], eye)
                last.then_inc(xqT_ready, 1)

            def up(c, half):
                if half:
                    pe.wait_ge(z_done, 2 * c + 1)
                else:
                    pe.wait_ge(xqT_copied, c + 1)
                for t in range(TILES):
                    for j in range(DC):
                        last = nc.tensor.matmul(bank_ff[:, t, :], xqT[:, t, j, :], w1T[:, j, half * 512:(half + 1) * 512],
                                                start=(j == 0), stop=(j == DC - 1))
                last.then_inc(up_ready, 1)

            def transpose_h(c, r):
                if r:
                    pe.wait_ge(hqT_copied, 2 * c + 1)
                else:
                    pe.wait_ge(hq_ready, c + 1)
                for t in range(TILES):
                    for j in range(4):
                        last = nc.tensor.transpose(bank_ff[:, t, j * P:(j + 1) * P], h[:, t, (4 * r + j) * P:(4 * r + j + 1) * P], eye)
                last.then_inc(hqT_ready, 1)

            def down(c):
                pe.wait_ge(hqT_copied, 2 * c + 2)
                for t in range(TILES):
                    for j in range(IC):
                        last = nc.tensor.matmul(bank_ff[:, t, 0:D], hqT[:, t, j, :], w2T[:, j, :],
                                                start=(j == 0), stop=(j == IC - 1))
                last.then_inc(down_ready, 1)

            def feed_forward_mid(c, k):
                if k == 3:
                    up(c, 0)
                if k == 7:
                    transpose_h(c, 0)

            def feed_forward_end(c, k):
                if k == 1:
                    attn_out(c)
                if k == 2:
                    transpose_x(c)
                if k == 3:
                    up(c, 1)
                if k == 7:
                    transpose_h(c, 1)
                    down(c)

            def body(b, first, last):
                for k in range(STEPS):
                    if first and k == 0:
                        pe.wait_ge(mask_made, 1)
                    scores(b, k)
                    if pair_in_step(b, k, last):
                        bb, j, s = pair_at(b, k)
                        project_pair(wcat[:, j, :, :], wswap[:, j, :], qcT[:, bass.ds(bb * S, S)], s)
                    if not (first and k < 2):
                        transpose_lat(*back(b, k, 2))
                    if not (first and k < 1):
                        transpose_probs(*back(b, k, 1))
                    if not first:
                        feed_forward_mid(b - 1, k)
                    if not (first and k < 1):
                        values(*back(b, k, 1))
                    if not first:
                        feed_forward_end(b - 1, k)

            run_batches(pe, body)
            transpose_lat(B - 1, STEPS - 2)
            transpose_probs(B - 1, STEPS - 1)
            values(B - 1, STEPS - 1)
            transpose_lat(B - 1, STEPS - 1)
            for k in range(STEPS):
                feed_forward_mid(B - 1, k)
                feed_forward_end(B - 1, k)

        @block.vector
        def _(dve):
            links = {"base": 0, "n": 0}

            def link(ins):
                links["n"] += 1
                ins.then_inc(dve_link, 1)
                dve.wait_ge(dve_link, links["base"] + links["n"])

            nc.vector.memset(ones[:, :], 1.0)
            nc.vector.memset(half_neg[:, :], -0.5)
            nc.vector.memset(kvc1[:, :, KVC:KVC + 1], 1.0)
            dve.wait_ge(in_sems["cst"], 16)
            nc.vector.tensor_copy(eye_b[:, :], eye).then_inc(consts_made, 1)

            def variance(src, width, ready):
                n = (width + 511) // 512
                for t in range(TILES):
                    for i in range(n):
                        lo = i * 512
                        last = nc.vector.bn_stats(stats[:, t, 6 * i:6 * i + 6], src(t)[:, lo:min(width, lo + 512)])
                link(last)
                nc.vector.memset(var[:, :], 0.0)
                for t in range(TILES):
                    last = nc.vector.bn_aggr(mv[:, t, :], stats[:, t, 0:6 * n])
                link(last)
                nc.vector.tensor_scalar(var[:, :], mv[:, :, 1], EPS, None, ALU.add).then_inc(ready, 1)

            dve.wait_ge(in_sems["x"], 16)
            dve.wait_ge(in_sems["ctx"], 16)

            def turn(dst, s, slot):
                dve.wait_ge(pair_ready, s + 1)
                nc.vector.tensor_tensor(dst, bank_pair[:, :].rearrange("p (e s) -> p e s", e=2), cos_tab, ALU.mult)
                if not (isinstance(s, int) and s < 2):
                    dve.wait_ge(pair_done, s - 1)
                nc.vector.tensor_tensor(turned[:, slot, :], bank_swap[:, 0:S], sin_tab, ALU.mult).then_inc(pair_turned, 1)

            for b in range(B):
                if b:
                    dve.wait_ge(xT_ready, b)
                variance(lambda t: x_all[:, b * TILES + t, :], D, a_var)
                dve.wait_ge(a_rstd, b + 1)
                for t in range(TILES):
                    last = nc.vector.tensor_scalar(xn[:, t, :], x_all[:, b * TILES + t, :], mv[:, t, 0:1], rstd[:, t:t + 1],
                                                   ALU.subtract, ALU.mult)
                last.then_inc(xn_ready, 1)
                dve.wait_ge(cT_ready, b + 1)
                if b:
                    dve.wait_ge(kvc_ready, b)
                nc.vector.tensor_copy(ctxT[:, :, :], bank_score[:, 1, :].rearrange("p (c s) -> p c s", c=DC)).then_inc(cT_copied, 1)
                if b:
                    dve.wait_ge(pair_done, b)
                turn(kcat[:, b, :, :], b, 0)

            dve.wait_ge(in_sems["seg"], 16)
            link(nc.vector.tensor_copy(seg_f[:, :], seg_i[:, :]))
            for i in range(B * TILES):
                d = dist[:, i % 2, :]
                link(nc.vector.tensor_scalar(d, iota, seg_f[:, i:i + 1], None, ALU.subtract))
                link(nc.vector.tensor_tensor(d, d, d, ALU.mult))
                last = nc.vector.tensor_scalar(mask[:, i, :], d, (LOOKBACK / 2) ** 2, NEG, ALU.is_gt, ALU.mult)
            last.then_inc(mask_made, 1)

            for i in range(H // 4):
                dve.wait_ge(fold_ready, i + 1)
                src = bank_prob[0:QC, 0:4 * KVC].rearrange("k (j e c) -> k j e c", e=2, c=KVC)
                nc.vector.tensor_copy(wcat[:, 2 * i:2 * i + 2, 0, 0:KVC], src[:, :, 0, :])
                nc.vector.tensor_copy(wcat[:, 2 * i:2 * i + 2, 1, R:P], src[:, :, 1, :]).then_inc(fold_copied, 1)
            for i in range(H // 4):
                dve.wait_ge(m_ready, i + 1)
                nc.vector.tensor_copy(m_sb[:, 2 * i:2 * i + 2, :],
                                      bank_ff[:, i % 2, :].rearrange("p (j n) -> p j n", j=2)).then_inc(m_copied, 1)

            dve.wait_ge(in_sems["w1"], 16)
            dve.wait_ge(in_sems["w2"], 16)
            nc.vector.tensor_reduce(wabs[:, 0:1], w1_sb[:, :, :], AX.XY, ALU.add, apply_absolute_value=True)
            nc.vector.tensor_reduce(wabs[:, 1:2], w2_sb[:, :, :], AX.XY, ALU.add, apply_absolute_value=True).then_inc(wabs_ready, 1)
            dve.wait_ge(wtot_ready, 1)
            link(nc.vector.tensor_scalar(wmean[:, :], bank_lat[:, 0:2], 1.0 / (INNER * D), 1e-5, ALU.mult, ALU.max))
            link(nc.vector.reciprocal(winv[:, :], wmean[:, :]))
            for i, (src, dst) in enumerate(((w1_sb[:, :, :].rearrange("p c n -> p (c n)"), w1q),
                                            (w2_sb[:, :, :].rearrange("p c n -> p (c n)"), w2q))):
                link(nc.vector.tensor_scalar(src, src, winv[:, i:i + 1], 1.0, ALU.mult, ALU.min))
                link(nc.vector.tensor_scalar(src, src, -1.0, MAGIC, ALU.max, ALU.add))
                last = nc.vector.tensor_scalar(dst[:, :], src, MAGIC, None, ALU.subtract)
            last.then_inc(wq_ready, 1)

            dve.wait_ge(pair_done, B)
            for j in range(AHEAD):
                turn(qcat[:, j, :, :], B + j, j % 2)

            def quantise(c, src, width, layer, sumsq_ready, ms, root, ready):
                nc.vector.tensor_reduce(amax[:, :], src[:, :, :], AX.X, ALU.max, apply_absolute_value=True)
                dve.wait_ge(sumsq_ready, c + 1)
                nc.vector.tensor_scalar(msq[:, :], sumsq[:, :], 1.0 / width, EPS, ALU.mult, ALU.add).then_inc(ms, 1)
                dve.wait_ge(root, c + 1)
                link(nc.vector.tensor_tensor(ymax[:, :], amax[:, :], rrms[:, :], ALU.mult))
                link(nc.vector.tensor_scalar(ymax[:, :], ymax[:, :], 1e-5, None, ALU.max))
                nc.vector.tensor_scalar(deq[:, layer, :], ymax[:, :], 1.0 / QMAX, wmean[:, layer:layer + 1], ALU.mult, ALU.mult)
                link(nc.vector.reciprocal(yinv[:, :], ymax[:, :]))
                link(nc.vector.scalar_tensor_tensor(qmul[:, :], yinv[:, :], QMAX, rrms[:, :], ALU.mult, ALU.mult))
                for t in range(TILES):
                    last = nc.vector.tensor_scalar(src[:, t, :], src[:, t, :], qmul[:, t:t + 1], MAGIC, ALU.mult, ALU.add)
                last.then_inc(ready, 1)

            def feed_forward(c, k):
                if k == 2:
                    dve.wait_ge(attn_ready, c + 1)
                    for t in range(TILES):
                        last = nc.vector.scalar_tensor_tensor(x1[:, t, :], bank_ff[:, t, 0:D], tgate[:, 0:1],
                                                              x_all[:, c * TILES + t, :], ALU.mult, ALU.add)
                    link(last)
                    variance(lambda t: x1[:, t, :], D, x_var)
                    dve.wait_ge(x_rstd, c + 1)
                    for t in range(TILES):
                        last = nc.vector.tensor_scalar(xl[:, t, :], x1[:, t, :], mv[:, t, 0:1], rstd[:, t:t + 1],
                                                       ALU.subtract, ALU.mult)
                    last.then_inc(xl_ready, 1)
                    dve.wait_ge(xl_ready, c + 1)
                    quantise(c, xl, D, 0, x_sumsq, x_ms, x_rrms, xq_ready)
                if k == 3:
                    for half in range(2):
                        dve.wait_ge(up_ready, 2 * c + half + 1)
                        for t in range(TILES):
                            last = nc.vector.scalar_tensor_tensor(h[:, t, half * 512:(half + 1) * 512], bank_ff[:, t, :],
                                                                  deq[:, 0, t:t + 1], b1_bc[:, half * 512:(half + 1) * 512],
                                                                  ALU.mult, ALU.add)
                        last.then_inc(z_done, 1)
                if k == 5:
                    dve.wait_ge(gelu_done, c + 1)
                    variance(lambda t: h[:, t, :], INNER, h_var)
                    dve.wait_ge(h_rstd, c + 1)
                    nc.vector.tensor_scalar(h[:, 1, :], h[:, 1, :], mv[:, 1, 0:1], rstd[:, 1:2],
                                            ALU.subtract, ALU.mult).then_inc(h_norm, 1)
                    link(nc.vector.scalar_tensor_tensor(h[:, 0, :], h[:, 0, :], mv[:, 0, 0:1], g_bc[:, :], ALU.subtract, ALU.mult))
                    nc.vector.scalar_tensor_tensor(h[:, 0, :], h[:, 0, :], rstd[:, 0:1], lb_bc[:, :],
                                                   ALU.mult, ALU.add).then_inc(h_ready0, 1)
                if k == 6:
                    dve.wait_ge(h_ready0, c + 1)
                    dve.wait_ge(h_ready1, c + 1)
                    quantise(c, h, INNER, 1, h_sumsq, h_ms, h_rrms, hq_ready)
                if k == 7:
                    dve.wait_ge(down_ready, c + 1)
                    for t in range(TILES):
                        last = nc.vector.scalar_tensor_tensor(ytmp[:, t, :], bank_ff[:, t, 0:D], deq[:, 1, t:t + 1],
                                                              b2_bc[:, :], ALU.mult, ALU.add)
                    link(last)
                    if not (isinstance(c, int) and c == 0):
                        dve.wait_ge(out_stored, 16 * c)
                    for t in range(TILES):
                        last = nc.vector.scalar_tensor_tensor(y[:, t, :], ytmp[:, t, :], tgate[:, 1:2], x1[:, t, :],
                                                              ALU.mult, ALU.add)
                    last.then_inc(y_done, 1)

            def softmax_shift(b, k):
                n = step_no(b, k)
                dve.wait_ge(score_ready, n + 1)
                src = bank_score[:, 0:KT, :].rearrange("p i s -> p (i s)").rearrange("p (h s) -> p h s", h=GROUP)
                nc.vector.tensor_reduce(smax[:, k % 2, :], src, AX.X, ALU.max).then_inc(smax_done, 1)
                if not (isinstance(b, int) and n < 2):
                    dve.wait_ge(probT_ready, (n - 1) * KT)
                dve.wait_ge(smax_done, n + 1)
                nc.vector.tensor_tensor(prob[:, k % 2, :, :], src,
                                        smax[:, k % 2, :].unsqueeze(2).broadcast_to([P, GROUP, KT * P]),
                                        ALU.subtract).then_inc(shifted, 1)

            def normalise(b, k):
                n = step_no(b, k)
                dve.wait_ge(lat_ready, n + 1)
                src = bank_lat[:, 0:GROUP * (KVC + 1)].rearrange("p (h c) -> p h c", h=GROUP)
                nc.vector.reciprocal(rsum[:, k % 2, :], src[:, :, KVC]).then_inc(rsum_done, 1)
                if not (isinstance(b, int) and n < 2):
                    dve.wait_ge(latT_ready, n - 1)
                dve.wait_ge(rsum_done, n + 1)
                nc.vector.tensor_tensor(lat[:, k % 2, :, :], src[:, :, 0:KVC],
                                        rsum[:, k % 2, :].unsqueeze(2).broadcast_to([P, GROUP, KVC]),
                                        ALU.mult).then_inc(lat_done, 1)

            def body(b, first, last):
                for k in range(STEPS):
                    softmax_shift(b, k)
                    if pair_in_step(b, k, last):
                        bb, j, s = pair_at(b, k)
                        if not (isinstance(bb, int) and bb == 0):
                            dve.wait_ge(score_ready, step_no(bb - 1, 2 * (j // 2) + 1) + 1)
                        turn(qcat[:, j, :, :], s, j % 2)
                    if not (first and k < 1):
                        normalise(*back(b, k, 1))
                    if not first:
                        feed_forward(b - 1, k)

            dve.wait_ge(gates_done, 1)
            for name in ("b1", "b2", "g", "lb"):
                dve.wait_ge(in_sems[name], 16)
            LINKS = 15
            body(0, True, False)
            start = links["n"]
            with dve.Fori(1, B - 1) as b:
                links["base"], links["n"] = start + (b - 1) * LINKS, 0
                body(b, False, False)
                assert links["n"] == LINKS, links["n"]
            links["base"], links["n"] = start + (B - 2) * LINKS, 0
            body(B - 1, False, True)
            normalise(B - 1, STEPS - 1)
            for k in range(STEPS):
                feed_forward(B - 1, k)


_INS = ['x', 'ctx_2048', 'itok_BxS_0_1023', 'g_xattn', 'g_ffn', 'L0_xattn_W_kvc', 'L0_xattn_W_dq',
        'L0_xattn_W_uq', 'L0_xattn_W_qr', 'L0_xattn_W_uk', 'L0_xattn_W_kr', 'L0_xattn_W_uv', 'L0_xattn_W_o',
        'L0_ffn_w1', 'L0_ffn_b1', 'L0_ffn_ln_g', 'L0_ffn_ln_b', 'L0_ffn_w2', 'L0_ffn_b2']


def kernel(**inputs):
    import numpy as _np
    import concourse.bacc as _bacc
    from concourse import mybir as _mybir
    from concourse.bass_utils import run_bass_kernel_spmd as _run

    nc = _bacc.Bacc("TRN2", target_bir_lowering=False, num_devices=1)
    arrays, args = {}, []
    for name in _INS:
        a = _np.ascontiguousarray(inputs[name])
        arrays[f"in_{name}"] = a
        args.append(nc.dram_tensor(f"in_{name}", a.shape, _mybir.dt.from_np(a.dtype), kind="ExternalInput").ap())
    c = shape_constants()
    arrays["in_consts"] = c
    args.append(nc.dram_tensor("in_consts", c.shape, _mybir.dt.from_np(c.dtype), kind="ExternalInput").ap())
    args.append(nc.dram_tensor("out_x", (B, S, D), _mybir.dt.float32, kind="ExternalOutput").ap())
    build(nc, *args)
    r = _run(nc, [arrays], core_ids=[0])
    return r.results[0]["out_x"]
```

```python
from contextlib import ExitStack

import numpy as np
import concourse.bass as bass
from concourse import mybir

B, S, D = 4, 256, 256
H, HD, R = 16, 128, 64
KVC, QC = 64, 96
INNER = 1024
LOOKBACK = 8
P = 128
TILES = S // P
DC = D // P
IC = INNER // P
PAIRS = H // 2
GROUP = 4
STEPS = H // GROUP
F = B * TILES
N = F * STEPS
AHEAD = 2
SCALE = float(1.0 / np.sqrt(np.float32(HD + R)))
NEG = -1e30
EPS = 1e-5
MAGIC = 12582912.0
QMAX = 127.0
EYE, IOTA, COS, SIN, CONSTS = 0, P, P + S, P + 3 * S, P + 4 * S


def shape_constants():
    half = R // 2
    freq = (np.float32(1.0) / np.float32(10000.0) ** (np.arange(half, dtype=np.float32) / np.float32(half)))
    ang = np.arange(S, dtype=np.float32)[None, :] * freq.astype(np.float32)[:, None]
    cos, sin = np.cos(ang).astype(np.float32), np.sin(ang).astype(np.float32)
    one = np.ones((KVC, S), np.float32)
    c = np.zeros((P, CONSTS), np.float32)
    c[:, EYE:EYE + P] = np.eye(P, dtype=np.float32)
    c[:, IOTA:IOTA + S] = np.arange(S, dtype=np.float32)[None, :] + LOOKBACK / 2
    c[:, COS:COS + S] = np.concatenate([one, cos, cos])
    c[:, COS + S:COS + 2 * S] = np.concatenate([cos, cos, one])
    c[:, SIN:SIN + S] = np.concatenate([-sin, sin, -sin, sin])
    return c


def build(nc, x, ctx_kv, itok, g_xattn, g_ffn, W_kvc, W_dq, W_uq, W_qr, W_uk, W_kr, W_uv, W_o,
          w1, b1, ln_g, ln_b, w2, b2, consts, out):
    fp32, bf16, i32 = mybir.dt.float32, mybir.dt.bfloat16, mybir.dt.int32
    ALU, ACT, AX = mybir.AluOpType, mybir.ActivationFunctionType, mybir.AxisListType
    KT = S // P

    with ExitStack() as stack:
        def sb(name, shape, dt=fp32):
            return stack.enter_context(nc.sbuf_tensor(name, shape, dt))

        def ps(name, shape, dt=fp32):
            return stack.enter_context(nc.psum_tensor(name, shape, dt))

        def sem(name):
            return stack.enter_context(nc.semaphore(name))

        x_all = sb("x_all", [P, F, D])
        ctx_all = sb("ctx_all", [P, F, D])
        seg_i = sb("seg_i", [P, F], i32)
        cst = sb("cst", [P, CONSTS])
        wdq = sb("wdq", [P, DC, QC])
        wkvc = sb("wkvc", [P, DC, KVC])
        wkr = sb("wkr", [KVC, R])
        wuq = sb("wuq", [QC, H, HD])
        wqr = sb("wqr", [QC, H, R])
        wuk_wuv = sb("wuk_wuv", [P, H, HD])
        wo = sb("wo", [HD, H, D])
        w1_sb = sb("w1_sb", [P, IC, D])
        w2_sb = sb("w2_sb", [P, DC, INNER])
        b1_bc = sb("b1_bc", [P, INNER])
        g_bc = sb("g_bc", [P, INNER])
        lb_bc = sb("lb_bc", [P, INNER])
        b2_bc = sb("b2_bc", [P, D])
        gates = sb("gates", [P, 2])
        wuk = wuk_wuv[0:KVC, :, :]

        wuqT = sb("wuqT", [HD, 2, 4, QC])
        wukT = sb("wukT", [HD, 2, 4, KVC])
        wuvT = sb("wuvT", [HD, H, KVC])
        wcat = sb("wcat", [QC, PAIRS, 2, P])
        wswap = sb("wswap", [QC, PAIRS, P])
        kcat_w = sb("kcat_w", [KVC, 2, P])
        kswap_w = sb("kswap_w", [KVC, P])
        m_sb = sb("m_sb", [P, PAIRS, D])
        w1T = sb("w1T", [P, DC, INNER], bf16)
        w2T = sb("w2T", [P, IC, D], bf16)
        w1q = sb("w1q", [P, IC * D], bf16)
        w2q = sb("w2q", [P, DC * INNER], bf16)

        eye_b = sb("eye_b", [P, P], bf16)
        ones = sb("ones", [P, P])
        half_neg = sb("half_neg", [P, F])
        eps = sb("eps", [P, F])
        inv_inner = sb("inv_inner", [P, 1])
        pad = sb("pad", [P, 1])
        mask = sb("mask", [P, F, S], bf16)
        seg_f = sb("seg_f", [P, F])
        far = sb("far", [P, F])
        farthest = sb("farthest", [P, 2])
        wide = sb("wide", [1, 1], i32)
        dist = sb("dist", [P, 2, S])
        tgate = sb("tgate", [P, 2])
        wabs = sb("wabs", [P, 2])
        wmean = sb("wmean", [P, 2])
        winv = sb("winv", [P, 2])

        prob_room = sb("prob_room", [P, 2 * GROUP * KT * P])
        xnT = prob_room[:, 0:DC * S].rearrange("p (c s) -> p c s", c=DC)
        ctxT = prob_room[:, DC * S:2 * DC * S].rearrange("p (c s) -> p c s", c=DC)
        probT_room = sb("probT_room", [P, 2 * KT * GROUP * P])
        xn = probT_room[:, :].rearrange("p (f n) -> p f n", f=F)
        a_stats = sb("a_stats", [P, F, 6])
        a_mv = sb("a_mv", [P, F, 2])
        a_var = sb("a_var", [P, F])
        a_root = sb("a_root", [P, F])
        qcT = sb("qcT", [QC, B * S])
        kvcT = sb("kvcT", [KVC, S])
        kcat = sb("kcat", [P, B, 2, S])
        kvc1 = sb("kvc1", [P, B * KT, KVC + 1])

        qcat = sb("qcat", [P, STEPS, 2, 2, P])
        turned = sb("turned", [P, 2, S])
        prob = prob_room[:, :].rearrange("p (n h s) -> p n h s", n=2, h=GROUP)
        probT = probT_room[:, :].rearrange("p (n t h s) -> p n t h s", n=2, t=KT, h=GROUP)
        neg_max = sb("neg_max", [P, 2, GROUP])
        rsum = sb("rsum", [P, 2, GROUP])
        lat = sb("lat", [P, 2, GROUP, KVC])
        latT = sb("latT", [P, PAIRS, P])

        x_stats = sb("x_stats", [P, 6])
        x_mv = sb("x_mv", [P, 2])
        x_small = sb("x_small", [P, 9])
        xl = sb("xl", [P, D])
        xqT = sb("xqT", [P, DC, P], bf16)
        z = sb("z", [P, INNER])
        h_stats = sb("h_stats", [P, 12])
        h_mv = sb("h_mv", [P, 2])
        h_small = sb("h_small", [P, 9])
        h = sb("h", [P, INNER])
        hqT = sb("hqT", [P, IC, P], bf16)
        junk = sb("junk", [P, INNER], bf16)
        ytmp = sb("ytmp", [P, D])
        y = sb("y", [P, D])
        VAR, RSTD, SQ, MS, RRMS, AMAX, YMAX, YINV, QMUL = range(9)
        x_deq = sb("x_deq", [P, 1])
        h_deq = sb("h_deq", [P, 1])

        def xs(i):
            return x_small[:, i:i + 1]

        def hs(i):
            return h_small[:, i:i + 1]

        bank_pair = ps("bank_pair", [P, 512])
        bank_swap = ps("bank_swap", [P, 512])
        bank_score = ps("bank_score", [P, 2, 512])
        bank_prob = ps("bank_prob", [P, 512])
        bank_lat = ps("bank_lat", [P, 512])
        bank_ff = ps("bank_ff", [P, 2, 512])

        in_sems = {n: sem("in_" + n) for n in (
            "x0", "x1", "ctx0", "ctx1", "seg", "eye", "rope", "wdq", "wkvc", "wkr", "wuq", "wqr", "wuk", "wuv",
            "wo", "w1", "w2", "b1", "g", "lb", "b2", "gate0", "gate1")}
        out_stored = sem("out_stored")
        consts_made = sem("consts_made")
        mask_made = sem("mask_made")
        far_ready = sem("far_ready")
        far_turned = sem("far_turned")
        wide_ready = sem("wide_ready")
        kweights = sem("kweights")
        wcopies = sem("wcopies")
        gates_done = sem("gates_done")
        a_var_ready = sem("a_var_ready")
        a_root_ready = sem("a_root_ready")
        xn_ready = sem("xn_ready")
        xT_ready = sem("xT_ready")
        xT_copied = sem("xT_copied")
        cT_ready = sem("cT_ready")
        cT_copied = sem("cT_copied")
        qc_ready = sem("qc_ready")
        qc_copied = sem("qc_copied")
        kvc_ready = sem("kvc_ready")
        kvc_copied = sem("kvc_copied")
        kvk_ready = sem("kvk_ready")
        kvk_copied = sem("kvk_copied")
        wt_ready = sem("wt_ready")
        wt_copied = sem("wt_copied")
        fold_ready = sem("fold_ready")
        fold_copied = sem("fold_copied")
        wuvT_ready = sem("wuvT_ready")
        wuvT_copied = sem("wuvT_copied")
        m_ready = sem("m_ready")
        m_copied = sem("m_copied")
        wabs_ready = sem("wabs_ready")
        wtot_ready = sem("wtot_ready")
        wq_ready = sem("wq_ready")
        wqT_ready = sem("wqT_ready")
        wqT_copied = sem("wqT_copied")
        pair_ready = sem("pair_ready")
        pair_turned = sem("pair_turned")
        pair_half = sem("pair_half")
        pair_done = sem("pair_done")
        score_ready = sem("score_ready")
        max_done = sem("max_done")
        exp_done = sem("exp_done")
        probT_ready = sem("probT_ready")
        probT_copied = sem("probT_copied")
        lat_ready = sem("lat_ready")
        rsum_done = sem("rsum_done")
        lat_done = sem("lat_done")
        latT_ready = sem("latT_ready")
        latT_copied = sem("latT_copied")
        attn_ready = sem("attn_ready")
        x1_done = sem("x1_done")
        x_moments = sem("x_moments")
        x_rstd = sem("x_rstd")
        x_rrms = sem("x_rrms")
        xq_ready = sem("xq_ready")
        xqT_ready = sem("xqT_ready")
        xqT_copied = sem("xqT_copied")
        up_ready = sem("up_ready")
        z_done = sem("z_done")
        silu_done = sem("silu_done")
        gelu_done = sem("gelu_done")
        h_moments = sem("h_moments")
        h_rstd = sem("h_rstd")
        h_ready = sem("h_ready")
        h_sumsq = sem("h_sumsq")
        h_rrms = sem("h_rrms")
        hq_ready = sem("hq_ready")
        hqT_ready = sem("hqT_ready")
        hqT_copied = sem("hqT_copied")
        down_ready = sem("down_ready")
        y_done = sem("y_done")
        dve_link = sem("dve_link")
        pool_link = sem("pool_link")

        eye = cst[:, EYE:EYE + P]
        iota = cst[:, IOTA:IOTA + S]
        cos_tab = cst[:, COS:COS + 2 * S].rearrange("p (e s) -> p e s", e=2)
        sin_tab = cst[:, SIN:SIN + S]

        def known(v):
            return isinstance(v, int)

        def behind(f, k, d):
            return (f, k - d) if k >= d else (f - 1, k - d + STEPS)

        def ahead(f, k):
            return (f, k + AHEAD) if k + AHEAD < STEPS else (f + 1, k + AHEAD - STEPS)

        def step_no(f, k):
            return f * STEPS + k

        def choose(eng, main):
            eng.wait_ge(wide_ready, 1)
            w = eng.value_load(wide[0:1, 0:1], min_val=0, max_val=1)
            with eng.If(w == 0):
                main(1)
            with eng.Else():
                main(KT)

        LEAD = 3

        def run_tiles(eng, body, before=lambda f: None):
            for f in range(LEAD):
                before(f)
                body(f)
            before(None)
            with eng.Fori(LEAD, F - 1) as f:
                before(f)
                body(f)
            for f in range(F - 1, F + LEAD):
                before(f)
                body(f)

        def there(f, lag):
            return not known(f) or 0 <= f - lag < F

        def score_banks(k, kts):
            banks = bank_score[:, k % 2, :] if kts == 1 else bank_score[:, :, :].rearrange("p i s -> p (i s)")
            return banks.rearrange("p (h s) -> p h s", h=GROUP)

        block = stack.enter_context(nc.Block())

        @block.sync
        def _(sp):
            def load(dst, src, name):
                sp.dma_start(dst, src).then_inc(in_sems[name], 16)

            x_v = x.rearrange("b (t p) d -> p (b t) d", p=P)
            load(cst[:, 0:COS], consts[:, 0:COS], "eye")
            load(x_all[:, 0:TILES, :], x_v[:, 0:TILES, :], "x0")
            load(wdq[:, :, :], W_dq.rearrange("(c p) n -> p c n", p=P), "wdq")
            load(x_all[:, TILES:F, :], x_v[:, TILES:F, :], "x1")
            load(wuq[:, :, :], W_uq.rearrange("k (h n) -> k h n", h=H), "wuq")
            load(wuk, W_uk.rearrange("k (h n) -> k h n", h=H), "wuk")
            load(wo[:, :, :], W_o.rearrange("(h p) n -> p h n", p=P), "wo")
            load(w2_sb[:, :, :], w2.rearrange("(c p) n -> p c n", p=P), "w2")
            load(g_bc[:, :], ln_g.partition_broadcast(P), "g")
            load(lb_bc[:, :], ln_b.partition_broadcast(P), "lb")
            load(b2_bc[:, :], b2.partition_broadcast(P), "b2")

            out_v = out.rearrange("b (t p) d -> (b t) p d", p=P)
            with sp.Fori(0, F) as f:
                sp.wait_ge(y_done, f + 1)
                sp.dma_start(out_v[bass.ds(f, 1), :, :].rearrange("o p d -> p (o d)"), y[:, :]).then_inc(out_stored, 16)
            sp.wait_ge(out_stored, 16 * F)

        @block.gpsimd
        def _(pool):
            half = R // 2
            pool.wait_ge(in_sems["eye"], 16)
            pool.wait_ge(in_sems["wkr"], 16)
            nc.gpsimd.tensor_copy(kcat_w[:, 0, 0:KVC], eye[0:KVC, 0:KVC])
            nc.gpsimd.tensor_copy(kcat_w[:, 0, KVC:P], wkr[:, :])
            nc.gpsimd.tensor_copy(kcat_w[:, 1, 0:R], wkr[:, :])
            nc.gpsimd.tensor_copy(kcat_w[:, 1, R:P], eye[0:KVC, 0:KVC])
            for o in (0, R):
                nc.gpsimd.tensor_copy(kswap_w[:, o:o + half], wkr[:, half:R])
                last = nc.gpsimd.tensor_copy(kswap_w[:, o + half:o + R], wkr[:, 0:half])
            last.then_inc(kweights, 1)
            pool.wait_ge(consts_made, 1)
            for i, (lo, hi) in enumerate(((0, TILES), (TILES, F))):
                pool.wait_ge(a_var_ready, i + 1)
                nc.gpsimd.tensor_tensor(a_root[:, lo:hi], a_var[:, lo:hi], half_neg[:, lo:hi], ALU.pow).then_inc(a_root_ready, 1)

            pool.wait_ge(in_sems["wqr"], 16)
            wqr_pair = wqr[:, :, :].rearrange("k (j e) n -> k j e n", e=2)
            nc.gpsimd.tensor_copy(wcat[:, :, 0, KVC:P], wqr_pair[:, :, 0, :])
            nc.gpsimd.tensor_copy(wcat[:, :, 1, 0:R], wqr_pair[:, :, 1, :])
            for o, e in ((0, 1), (R, 0)):
                nc.gpsimd.tensor_copy(wswap[:, :, o:o + half], wqr_pair[:, :, e, half:R])
                last = nc.gpsimd.tensor_copy(wswap[:, :, o + half:o + R], wqr_pair[:, :, e, 0:half])
            last.then_inc(wcopies, 1)

            def add_rope(even, odd, add_even, add_odd, s):
                pool.wait_ge(pair_turned, s + 1)
                nc.gpsimd.tensor_tensor(odd, odd, add_odd, ALU.add).then_inc(pair_half, 1)
                pool.wait_ge(pair_half, s + 1)
                nc.gpsimd.tensor_tensor(even, even, add_even, ALU.add).then_inc(pair_done, 1)
                pool.wait_ge(pair_done, s + 1)

            with pool.Fori(0, B) as b:
                add_rope(kcat[KVC:P, b, 0, :], kcat[0:R, b, 1, :], turned[KVC:P, 0, :], turned[0:R, 0, :], b)

            def add_rope_step(f, k):
                t = turned[:, k % 2, :].rearrange("p (j s) -> p j s", j=2)
                add_rope(qcat[KVC:P, k, :, 0, :], qcat[0:R, k, :, 1, :], t[KVC:P, :, :], t[0:R, :, :], B + step_no(f, k))

            for k in range(AHEAD):
                add_rope_step(0, k)

            links = {"base": 0, "n": 0}

            def link(ins):
                links["n"] += 1
                ins.then_inc(pool_link, 1)
                pool.wait_ge(pool_link, links["base"] + links["n"])

            def small(dst, a, b, op):
                return nc.gpsimd.tensor_tensor(dst, a, b, op)

            pow_half, eps1 = half_neg[:, 0:1], eps[:, 0:1]

            def feed_forward(f, k):
                if k == 1 and there(f, 3):
                    pool.wait_ge(h_sumsq, f - 2)
                    link(small(hs(MS), hs(SQ), inv_inner[:, :], ALU.mult))
                    link(small(hs(MS), hs(MS), eps1, ALU.add))
                    small(hs(RRMS), hs(MS), pow_half, ALU.pow).then_inc(h_rrms, 1)
                if k == 2 and there(f, 1):
                    pool.wait_ge(x_moments, f)
                    link(small(xs(VAR), x_mv[:, 1:2], eps1, ALU.add))
                    small(xs(RSTD), xs(VAR), pow_half, ALU.pow).then_inc(x_rstd, 1)
                    pool.wait_ge(x_rstd, f)
                    link(small(xs(SQ), xs(RSTD), xs(RSTD), ALU.mult))
                    link(small(xs(MS), xs(SQ), x_mv[:, 1:2], ALU.mult))
                    link(small(xs(MS), xs(MS), eps1, ALU.add))
                    small(xs(RRMS), xs(MS), pow_half, ALU.pow).then_inc(x_rrms, 1)
                if k == 3 and there(f, 2):
                    pool.wait_ge(h_moments, f - 1)
                    link(small(hs(VAR), h_mv[:, 1:2], eps1, ALU.add))
                    small(hs(RSTD), hs(VAR), pow_half, ALU.pow).then_inc(h_rstd, 1)

            LINKS = 7

            def before(f):
                if f is None:
                    links["start"] = links["base"] + links["n"]
                    return
                if known(f):
                    if f == F - 1:
                        links["base"], links["n"] = links["start"] + (F - 1 - LEAD) * LINKS, 0
                else:
                    links["base"], links["n"] = links["start"] + (f - LEAD) * LINKS, 0

            def body(f):
                for k in range(STEPS):
                    if not known(f) or step_no(f, k) + AHEAD < N:
                        add_rope_step(*ahead(f, k))
                    feed_forward(f, k)
                assert known(f) or links["n"] == LINKS, links["n"]

            run_tiles(pool, body, before)

        @block.scalar
        def _(act):
            def load(dst, src, name):
                act.dma_start(dst, src).then_inc(in_sems[name], 16)

            ctx_v = ctx_kv.rearrange("b (t p) d -> p (b t) d", p=P)
            load(ctx_all[:, 0:TILES, :], ctx_v[:, 0:TILES, :], "ctx0")
            load(wkvc[:, :, :], W_kvc.rearrange("(c p) n -> p c n", p=P), "wkvc")
            load(wkr[:, :], W_kr, "wkr")
            load(ctx_all[:, TILES:F, :], ctx_v[:, TILES:F, :], "ctx1")
            load(cst[:, COS:CONSTS], consts[:, COS:CONSTS], "rope")
            with nc.allow_non_contiguous_dma(reason="1024 token numbers"):
                load(seg_i[:, :], itok.rearrange("b (t p) -> p (b t)", p=P), "seg")
            load(wqr[:, :, :], W_qr.rearrange("k (h n) -> k h n", h=H), "wqr")
            load(gates[:, 0:1], g_xattn.partition_broadcast(P), "gate0")
            load(gates[:, 1:2], g_ffn.partition_broadcast(P), "gate1")
            load(wuk_wuv[KVC:P, :, :], W_uv.rearrange("k (h n) -> k h n", h=H), "wuv")
            load(w1_sb[:, :, :], w1.rearrange("(c p) n -> p c n", p=P), "w1")
            load(b1_bc[:, :], b1.partition_broadcast(P), "b1")

            act.wait_ge(consts_made, 1)
            for b in range(B):
                act.wait_ge(xT_ready, b + 1)
                nc.scalar.copy(xnT, bank_score[:, 0, :].rearrange("p (c s) -> p c s", c=DC)).then_inc(xT_copied, 1)
                act.wait_ge(kvc_ready, b + 1)
                nc.scalar.copy(kvcT[:, :], bank_lat[0:KVC, 0:S]).then_inc(kvc_copied, 1)
                act.wait_ge(qc_ready, b + 1)
                nc.scalar.activation(qcT[:, b * S:(b + 1) * S], bank_prob[0:QC, 0:S], ACT.Copy,
                                     scale=SCALE).then_inc(qc_copied, 1)
                act.wait_ge(kvk_ready, b + 1)
                nc.scalar.copy(kvc1[:, b * KT:(b + 1) * KT, 0:KVC],
                               bank_ff[:, 0, 0:KT * KVC].rearrange("p (t c) -> p t c", t=KT)).then_inc(kvk_copied, 1)

            act.wait_ge(in_sems["gate0"], 16)
            act.wait_ge(in_sems["gate1"], 16)
            nc.scalar.activation(tgate[:, :], gates[:, :], ACT.Tanh).then_inc(gates_done, 1)

            for i in range(H // 4):
                act.wait_ge(wt_ready, i + 1)
                if i >= 2:
                    act.wait_ge(fold_ready, i - 1)
                nc.scalar.copy(wuqT[:, i % 2, :, :], bank_score[:, 0, 0:4 * QC].rearrange("p (h c) -> p h c", h=4))
                nc.scalar.copy(wukT[:, i % 2, :, :],
                               bank_score[:, 1, 0:4 * KVC].rearrange("p (h c) -> p h c", h=4)).then_inc(wt_copied, 1)

            def prepare(f, k):
                if known(f) and f == 0 and k < 2:
                    act.wait_ge(wuvT_ready, k + 1)
                    nc.scalar.copy(wuvT[:, 8 * k:8 * k + 8, :],
                                   bank_ff[:, k, :].rearrange("p (h c) -> p h c", h=8)).then_inc(wuvT_copied, 1)
                if known(f) and f == 1:
                    act.wait_ge(wqT_ready, k + 1)
                    src = bank_ff[:, 1, :].bitcast(bf16)
                    dst = w1T[:, k, :] if k < 2 else w2T[:, 4 * (k - 2):4 * (k - 1), :]
                    if k >= 2:
                        src = src.rearrange("p (c n) -> p c n", c=4)
                    nc.scalar.copy(dst, src).then_inc(wqT_copied, 1)

            def feed_forward_start(f, k):
                if k == 0 and there(f, 2):
                    act.wait_ge(xqT_ready, f - 1)
                    nc.scalar.activation(xqT[:, :, :], bank_ff[:, 1, 0:D].rearrange("p (c s) -> p c s", c=DC),
                                         ACT.Copy, bias=-MAGIC).then_inc(xqT_copied, 1)
                if k == 3 and there(f, 3):
                    copy_h(f, 1)

            def copy_h(f, r):
                act.wait_ge(hqT_ready, 2 * (f - 3) + r + 1)
                nc.scalar.activation(hqT[:, 4 * r:4 * r + 4, :], bank_ff[:, 1 - r, :].rearrange("p (c s) -> p c s", c=4),
                                     ACT.Copy, bias=-MAGIC).then_inc(hqT_copied, 1)

            def feed_forward_end(f, k):
                if k == 1 and there(f, 2):
                    act.wait_ge(z_done, f - 1)
                    nc.scalar.activation(z[:, :], z[:, :], ACT.Silu).then_inc(silu_done, 1)
                    act.wait_ge(silu_done, f - 1)
                    nc.scalar.activation(z[:, :], z[:, :], ACT.Gelu).then_inc(gelu_done, 1)
                if k == 2 and there(f, 3):
                    copy_h(f, 0)

            def sum_squares(f):
                act.wait_ge(h_ready, f - 2)
                nc.scalar.activation(junk[:, :], h[:, :], ACT.Square, accum_out=hs(SQ)).then_inc(h_sumsq, 1)

            def copy_latT(f, k):
                n = step_no(f, k)
                act.wait_ge(latT_ready, n + 1)
                if not (known(f) and f == 0):
                    act.wait_ge(attn_ready, f)
                nc.scalar.copy(latT[:, 2 * k:2 * k + 2, :],
                               bank_lat[:, 0:2 * P].rearrange("p (j s) -> p j s", j=2)).then_inc(latT_copied, 1)

            def copy_probT(f, k, kts):
                n = step_no(f, k)
                if not (known(n) and n < 2):
                    act.wait_ge(lat_ready, n - 1)
                for kt in range(kts):
                    act.wait_ge(probT_ready, n * kts + kt + 1)
                    nc.scalar.copy(probT[:, k % 2, kt, :, :],
                                   bank_prob[:, :].rearrange("p (h s) -> p h s", h=GROUP)).then_inc(probT_copied, 1)

            def exponentials(f, k, kts):
                n = step_no(f, k)
                src = score_banks(k, kts)
                act.wait_ge(max_done, n + 1)
                if not (known(n) and n < 2):
                    act.wait_ge(probT_ready, (n - 1) * kts)
                for j in range(GROUP):
                    last = nc.scalar.activation(prob[:, k % 2, j, 0:kts * P], src[:, j, :], ACT.Exp,
                                                bias=neg_max[:, k % 2, j:j + 1])
                last.then_inc(exp_done, 1)

            def main(kts):
                def body(f):
                    for k in range(STEPS):
                        feed_forward_start(f, k)
                        if not known(f) or 2 <= step_no(f, k) < N + 2:
                            copy_latT(*behind(f, k, 2))
                        if not known(f) or 1 <= step_no(f, k) < N + 1:
                            copy_probT(*behind(f, k, 1), kts)
                        if k == 1 and there(f, 3):
                            sum_squares(f)
                        if not known(f) or f < F:
                            exponentials(f, k, kts)
                        prepare(f, k)
                        feed_forward_end(f, k)

                run_tiles(act, body)

            choose(act, main)

        @block.tensor
        def _(pe):
            pe.wait_ge(in_sems["eye"], 16)
            for b in range(B):
                pe.wait_ge(in_sems["ctx0" if b == 0 else "ctx1"], 16)
                if b:
                    pe.wait_ge(cT_copied, b)
                for t in range(TILES):
                    for c in range(DC):
                        last = nc.tensor.transpose(bank_score[:, 1, c * S + t * P:c * S + (t + 1) * P],
                                                   ctx_all[:, b * TILES + t, c * P:(c + 1) * P], eye)
                last.then_inc(cT_ready, 1)
                pe.wait_ge(xn_ready, 1 if b == 0 else 2)
                if b:
                    pe.wait_ge(xT_copied, b)
                for t in range(TILES):
                    for c in range(DC):
                        last = nc.tensor.transpose(bank_score[:, 0, c * S + t * P:c * S + (t + 1) * P],
                                                   xn[:, b * TILES + t, c * P:(c + 1) * P], eye)
                last.then_inc(xT_ready, 1)
                if b == 0:
                    pe.wait_ge(in_sems["wkvc"], 16)
                    pe.wait_ge(in_sems["wdq"], 16)
                pe.wait_ge(cT_copied, b + 1)
                if b:
                    pe.wait_ge(kvc_copied, b)
                for c in range(DC):
                    last = nc.tensor.matmul(bank_lat[0:KVC, 0:S], wkvc[:, c, :], ctxT[:, c, :], start=(c == 0), stop=(c == DC - 1))
                last.then_inc(kvc_ready, 1)
                pe.wait_ge(xT_copied, b + 1)
                if b:
                    pe.wait_ge(qc_copied, b)
                for c in range(DC):
                    last = nc.tensor.matmul(bank_prob[0:QC, 0:S], wdq[:, c, :], xnT[:, c, :], start=(c == 0), stop=(c == DC - 1))
                last.then_inc(qc_ready, 1)
                pe.wait_ge(kvc_copied, b + 1)
                if b:
                    pe.wait_ge(pair_turned, b)
                else:
                    pe.wait_ge(kweights, 1)
                for e in range(2):
                    nc.tensor.matmul(bank_pair[:, e * S:(e + 1) * S], kcat_w[:, e, :], kvcT[:, :], start=True, stop=True)
                nc.tensor.matmul(bank_swap[:, 0:S], kswap_w[:, :], kvcT[:, :], start=True, stop=True).then_inc(pair_ready, 1)
                if b:
                    pe.wait_ge(kvk_copied, b)
                for kt in range(KT):
                    last = nc.tensor.transpose(bank_ff[:, 0, kt * KVC:(kt + 1) * KVC], kvcT[:, kt * P:(kt + 1) * P],
                                               eye[0:KVC, 0:KVC])
                last.then_inc(kvk_ready, 1)

            pe.wait_ge(in_sems["wuq"], 16)
            pe.wait_ge(in_sems["wuk"], 16)
            pe.wait_ge(xT_copied, B)
            pe.wait_ge(cT_copied, B)
            pe.wait_ge(qc_copied, B)

            def transpose_weights(i):
                if i:
                    pe.wait_ge(wt_copied, i)
                for j in range(4):
                    nc.tensor.transpose(bank_score[:, 0, j * QC:(j + 1) * QC], wuq[:, 4 * i + j, :], eye[0:QC, 0:QC])
                    last = nc.tensor.transpose(bank_score[:, 1, j * KVC:(j + 1) * KVC], wuk[:, 4 * i + j, :], eye[0:KVC, 0:KVC])
                last.then_inc(wt_ready, 1)

            transpose_weights(0)
            for i in range(H // 4):
                if i + 1 < H // 4:
                    transpose_weights(i + 1)
                pe.wait_ge(wt_copied, i + 1)
                if i:
                    pe.wait_ge(fold_copied, i)
                for j in range(4):
                    last = nc.tensor.matmul(bank_prob[0:QC, j * KVC:(j + 1) * KVC], wuqT[:, i % 2, j, :], wukT[:, i % 2, j, :],
                                            start=True, stop=True)
                last.then_inc(fold_ready, 1)
            pe.wait_ge(far_ready, 1)
            pe.wait_ge(kvk_copied, B)
            nc.tensor.matmul(bank_ff[0:1, 0, 0:P], farthest[:, 0:1], eye, start=True, stop=True).then_inc(far_turned, 1)

            def project(f, k):
                s = B + step_no(f, k)
                pe.wait_ge(pair_turned, s)
                src = qcT[:, bass.ds(f * P, P)]
                for j in range(2):
                    for e in range(2):
                        nc.tensor.matmul(bank_pair[:, (2 * j + e) * P:(2 * j + e + 1) * P], wcat[:, 2 * k + j, e, :], src,
                                         start=True, stop=True)
                for j in range(2):
                    last = nc.tensor.matmul(bank_swap[:, j * P:(j + 1) * P], wswap[:, 2 * k + j, :], src, start=True, stop=True)
                last.then_inc(pair_ready, 1)

            pe.wait_ge(wcopies, 1)
            pe.wait_ge(fold_copied, H // 4)
            for k in range(AHEAD):
                project(0, k)

            def prepare_mid(f, k):
                if known(f) and f == 0 and k == 0:
                    pe.wait_ge(in_sems["wuv"], 16)
                    pe.wait_ge(wide_ready, 1)
                    for i in range(H // 8):
                        for j in range(8):
                            last = nc.tensor.transpose(bank_ff[:, i, j * KVC:(j + 1) * KVC], wuk_wuv[KVC:P, 8 * i + j, :],
                                                       eye[KVC:P, KVC:P])
                        last.then_inc(wuvT_ready, 1)

            def prepare_end(f, k):
                if known(f) and f == 0:
                    if k == 1:
                        pe.wait_ge(in_sems["wo"], 16)
                        pe.wait_ge(wuvT_copied, 2)
                    if k in (1, 2):
                        for i in (2 * k - 2, 2 * k - 1):
                            if i >= 2:
                                pe.wait_ge(m_copied, i - 1)
                            for j in range(4):
                                hh = 4 * i + j
                                last = nc.tensor.matmul(bank_ff[(j % 2) * KVC:(j % 2 + 1) * KVC, i % 2, (j // 2) * D:(j // 2 + 1) * D],
                                                        wuvT[:, hh, :], wo[:, hh, :], start=True, stop=True)
                            last.then_inc(m_ready, 1)
                    if k == 3:
                        pe.wait_ge(wabs_ready, 1)
                        pe.wait_ge(m_copied, H // 4)
                        nc.tensor.matmul(bank_ff[:, 1, 0:2], ones[:, :], wabs[:, :], start=True, stop=True).then_inc(wtot_ready, 1)

            def transpose_ternary(f, k):
                if known(f) and f == 1:
                    pe.wait_ge(wq_ready, 1 if k < 2 else 2)
                    if k:
                        pe.wait_ge(wqT_copied, k)
                    dst = bank_ff[:, 1, :].bitcast(bf16)
                    for j in range(8):
                        if k < 2:
                            src = w1q[:, j * D + k * P:j * D + (k + 1) * P]
                        else:
                            ic, dc = 4 * (k - 2) + j // 2, j % 2
                            src = w2q[:, dc * INNER + ic * P:dc * INNER + (ic + 1) * P]
                        last = nc.tensor.transpose(dst[:, j * P:(j + 1) * P], src, eye_b[:, :])
                    last.then_inc(wqT_ready, 1)

            def scores(f, k, kts):
                n = step_no(f, k)
                lag = 1 if kts == 1 else 0
                if not (known(n) and n <= lag):
                    pe.wait_ge(exp_done, n - lag)
                pe.wait_ge(pair_done, B + n + 1)
                per = GROUP // kts
                b = f // TILES
                for i in range(kts):
                    bank = bank_score[:, k % 2 if kts == 1 else i, :]
                    nc.tensor.matmul(bank.rearrange("p (h s) -> p h s", h=per), eye_b[:, :],
                                     mask[:, bass.ds(f, 1), 0:kts * P].broadcast_to([P, per, kts * P]),
                                     start=True, stop=False, skip_group_check=True)
                    for j in range(per):
                        hh = per * i + j
                        last = nc.tensor.matmul(bank[:, j * kts * P:(j + 1) * kts * P],
                                                qcat[:, k, hh // 2, hh % 2, :], kcat[:, b, hh % 2, 0:kts * P],
                                                start=False, stop=(j == per - 1), skip_group_check=True)
                last.then_inc(score_ready, 1)

            def transpose_probs(f, k, kts):
                n = step_no(f, k)
                pe.wait_ge(exp_done, n + 1)
                for kt in range(kts):
                    if not (known(n) and n * kts + kt == 0):
                        pe.wait_ge(probT_copied, n * kts + kt)
                    for j in range(GROUP):
                        last = nc.tensor.transpose(bank_prob[:, j * P:(j + 1) * P], prob[:, k % 2, j, kt * P:(kt + 1) * P], eye)
                    last.then_inc(probT_ready, 1)

            def values(f, k, kts):
                n = step_no(f, k)
                b = f // TILES
                pe.wait_ge(probT_copied, (n + 1) * kts)
                if not (known(n) and n == 0):
                    pe.wait_ge(latT_copied, n)
                for j in range(GROUP):
                    for kt in range(kts):
                        last = nc.tensor.matmul(bank_lat[:, j * (KVC + 1):(j + 1) * (KVC + 1)], probT[:, k % 2, kt, j, :],
                                                kvc1[:, b * KT + kt, :], start=(kt == 0), stop=(kt == kts - 1))
                last.then_inc(lat_ready, 1)

            def transpose_lat(f, k):
                pe.wait_ge(lat_done, step_no(f, k) + 1)
                for j in range(2):
                    last = nc.tensor.transpose(bank_lat[:, j * P:(j + 1) * P],
                                               lat[:, k % 2, 2 * j:2 * j + 2, :].rearrange("p h c -> p (h c)"), eye)
                last.then_inc(latT_ready, 1)

            def attn_out(c):
                pe.wait_ge(latT_copied, (c + 1) * STEPS)
                if known(c) and c == 0:
                    pe.wait_ge(m_copied, H // 4)
                else:
                    pe.wait_ge(z_done, c)
                for j in range(PAIRS):
                    last = nc.tensor.matmul(bank_ff[:, 0, 0:D], latT[:, j, :], m_sb[:, j, :],
                                            start=(j == 0), stop=(j == PAIRS - 1))
                last.then_inc(attn_ready, 1)

            def transpose_x(c):
                pe.wait_ge(xq_ready, c + 1)
                if known(c) and c == 0:
                    pe.wait_ge(wqT_copied, 4)
                for j in range(DC):
                    last = nc.tensor.transpose(bank_ff[:, 1, j * P:(j + 1) * P], xl[:, j * P:(j + 1) * P], eye)
                last.then_inc(xqT_ready, 1)

            def up(c):
                pe.wait_ge(xqT_copied, c + 1)
                if not (known(c) and c < 2):
                    pe.wait_ge(y_done, c - 1)
                for half in range(2):
                    for j in range(DC):
                        last = nc.tensor.matmul(bank_ff[:, half, :], xqT[:, j, :], w1T[:, j, half * 512:(half + 1) * 512],
                                                start=(j == 0), stop=(j == DC - 1))
                last.then_inc(up_ready, 1)

            def transpose_h(c, r, f):
                if r:
                    if there(f, 1):
                        pe.wait_ge(x1_done, f)
                    else:
                        pe.wait_ge(z_done, c + 1 if c + 1 == F else c + 2)
                else:
                    pe.wait_ge(hq_ready, c + 1)
                    pe.wait_ge(z_done, F if known(c) and c + 2 > F else c + 2)
                for j in range(4):
                    last = nc.tensor.transpose(bank_ff[:, 1 - r, j * P:(j + 1) * P], h[:, (4 * r + j) * P:(4 * r + j + 1) * P], eye)
                last.then_inc(hqT_ready, 1)

            def down(c):
                pe.wait_ge(hqT_copied, 2 * c + 2)
                for j in range(IC):
                    last = nc.tensor.matmul(bank_ff[:, 0, 0:D], hqT[:, j, :], w2T[:, j, :], start=(j == 0), stop=(j == IC - 1))
                last.then_inc(down_ready, 1)

            def feed_forward_mid(f, k):
                if k == 2 and there(f, 3):
                    transpose_h(f - 3, 0, f)
                if k == 3 and there(f, 3):
                    transpose_h(f - 3, 1, f)

            def feed_forward_end(f, k):
                if k == 0 and there(f, 2):
                    up(f - 2)
                if k == 1 and there(f, 1):
                    attn_out(f - 1)
                if k == 3 and there(f, 3):
                    down(f - 3)
                if k == 3 and there(f, 1):
                    transpose_x(f - 1)

            def main(kts):
                def body(f):
                    for k in range(STEPS):
                        n = step_no(f, k)
                        if known(n) and n == 0:
                            pe.wait_ge(mask_made, 1)
                        if not known(f) or f < F:
                            scores(f, k, kts)
                        if not known(f) or 2 <= n < N + 2:
                            transpose_lat(*behind(f, k, 2))
                        if not known(f) or 1 <= n < N + 1:
                            transpose_probs(*behind(f, k, 1), kts)
                        if not known(f) or n + AHEAD < N:
                            project(*ahead(f, k))
                        prepare_mid(f, k)
                        if k == STEPS - 1:
                            transpose_ternary(f, k)
                        feed_forward_mid(f, k)
                        if not known(f) or 1 <= n < N + 1:
                            values(*behind(f, k, 1), kts)
                        feed_forward_end(f, k)
                        prepare_end(f, k)
                        if k < STEPS - 1:
                            transpose_ternary(f, k)

                run_tiles(pe, body)

            choose(pe, main)

        @block.vector
        def _(dve):
            links = {"base": 0, "n": 0}

            def link(ins):
                links["n"] += 1
                ins.then_inc(dve_link, 1)
                dve.wait_ge(dve_link, links["base"] + links["n"])

            nc.vector.memset(ones[:, :], 1.0)
            nc.vector.memset(half_neg[:, :], -0.5)
            nc.vector.memset(eps[:, :], EPS)
            nc.vector.memset(inv_inner[:, :], 1.0 / INNER)
            nc.vector.memset(kvc1[:, :, KVC:KVC + 1], 1.0)
            dve.wait_ge(in_sems["eye"], 16)
            nc.vector.tensor_copy(eye_b[:, :], eye).then_inc(consts_made, 1)

            def input_moments(i, lo, hi):
                dve.wait_ge(in_sems["x0" if lo == 0 else "x1"], 16)
                for f in range(lo, hi):
                    last = nc.vector.bn_stats(a_stats[:, f, :], x_all[:, f, :])
                link(last)
                for f in range(lo, hi):
                    last = nc.vector.bn_aggr(a_mv[:, f, :], a_stats[:, f, :])
                link(last)
                nc.vector.tensor_scalar(a_var[:, lo:hi], a_mv[:, lo:hi, 1], EPS, None, ALU.add).then_inc(a_var_ready, 1)

            def input_norm(i, lo, hi):
                dve.wait_ge(a_root_ready, i + 1)
                for f in range(lo, hi):
                    last = nc.vector.tensor_scalar(xn[:, f, :], x_all[:, f, :], a_mv[:, f, 0:1], a_root[:, f:f + 1],
                                                   ALU.subtract, ALU.mult)
                last.then_inc(xn_ready, 1)

            def turn(dst, cos, swapped, sin, slot, s):
                dve.wait_ge(pair_ready, s + 1)
                nc.vector.tensor_tensor(dst, bank_pair[:, :], cos, ALU.mult)
                nc.vector.tensor_tensor(turned[:, slot, :].rearrange("p (j s) -> p j s", j=2) if len(sin.shape) == 3 else turned[:, slot, :],
                                        swapped, sin, ALU.mult).then_inc(pair_turned, 1)

            def input_keys(b):
                dve.wait_ge(cT_ready, b + 1)
                if b:
                    dve.wait_ge(kvc_ready, b)
                nc.vector.tensor_copy(ctxT, bank_score[:, 1, :].rearrange("p (c s) -> p c s", c=DC)).then_inc(cT_copied, 1)

            def turn_keys(b):
                dve.wait_ge(pair_ready, b + 1)
                nc.vector.tensor_tensor(kcat[:, b, :, :], bank_pair[:, :].rearrange("p (e s) -> p e s", e=2), cos_tab, ALU.mult)
                if b:
                    dve.wait_ge(pair_done, b)
                nc.vector.tensor_tensor(turned[:, 0, :], bank_swap[:, 0:S], sin_tab, ALU.mult).then_inc(pair_turned, 1)

            input_moments(0, 0, TILES)
            input_norm(0, 0, TILES)
            input_keys(0)
            input_moments(1, TILES, F)
            dve.wait_ge(in_sems["rope"], 16)
            turn_keys(0)
            input_norm(1, TILES, F)
            for b in range(1, B):
                input_keys(b)
                turn_keys(b)

            mid = (P - 1) / 2
            dve.wait_ge(in_sems["seg"], 16)
            link(nc.vector.tensor_copy(seg_f[:, :], seg_i[:, :]))
            link(nc.vector.tensor_scalar(far[:, :], seg_f[:, :], mid, None, ALU.subtract))
            link(nc.vector.tensor_tensor(far[:, :], far[:, :], far[:, :], ALU.mult))
            nc.vector.tensor_reduce(farthest[:, 0:1], far[:, :], AX.X, ALU.max).then_inc(far_ready, 1)

            for i in range(F):
                d = dist[:, i % 2, :]
                link(nc.vector.tensor_scalar(d, iota, seg_f[:, i:i + 1], None, ALU.subtract))
                link(nc.vector.tensor_tensor(d, d, d, ALU.mult))
                last = nc.vector.tensor_scalar(mask[:, i, :], d, (LOOKBACK / 2) ** 2, NEG, ALU.is_gt, ALU.mult)
            last.then_inc(mask_made, 1)

            for i in range(H // 4):
                dve.wait_ge(fold_ready, i + 1)
                src = bank_prob[0:QC, 0:4 * KVC].rearrange("k (j e c) -> k j e c", e=2, c=KVC)
                nc.vector.tensor_copy(wcat[:, 2 * i:2 * i + 2, 0, 0:KVC], src[:, :, 0, :])
                nc.vector.tensor_copy(wcat[:, 2 * i:2 * i + 2, 1, R:P], src[:, :, 1, :]).then_inc(fold_copied, 1)
            dve.wait_ge(far_turned, 1)
            link(nc.vector.tensor_reduce(farthest[0:1, 1:2], bank_ff[0:1, 0, 0:P], AX.X, ALU.max))
            nc.vector.tensor_scalar(wide[:, :], farthest[0:1, 1:2], mid * mid, None, ALU.is_gt).then_inc(wide_ready, 1)

            def turn_step(f, k):
                s = B + step_no(f, k)
                at = (f % TILES) * P
                cos = cos_tab[:, :, bass.ds(at, P)].unsqueeze(1).broadcast_to([P, 2, 2, P])
                sin = sin_tab[:, bass.ds(at, P)].unsqueeze(1).broadcast_to([P, 2, P])
                dve.wait_ge(pair_ready, s + 1)
                if not (known(f) and f == 0):
                    dve.wait_ge(score_ready, step_no(f, k) - STEPS + 1)
                nc.vector.tensor_tensor(qcat[:, k, :, :, :], bank_pair[:, :].rearrange("p (j e s) -> p j e s", j=2, e=2),
                                        cos, ALU.mult)
                dve.wait_ge(pair_done, B if known(f) and step_no(f, k) < 2 else s - 1)
                nc.vector.tensor_tensor(turned[:, k % 2, :].rearrange("p (j s) -> p j s", j=2),
                                        bank_swap[:, 0:S].rearrange("p (j s) -> p j s", j=2), sin, ALU.mult).then_inc(pair_turned, 1)

            for k in range(AHEAD):
                turn_step(0, k)

            def prepare(f, k):
                if not known(f):
                    return
                if f == 0 and k == 0:
                    dve.wait_ge(in_sems["w1"], 16)
                    nc.vector.tensor_reduce(wabs[:, 0:1], w1_sb[:, :, :], AX.XY, ALU.add, apply_absolute_value=True)
                if f == 0 and k in (1, 2):
                    for i in (2 * k - 2, 2 * k - 1):
                        dve.wait_ge(m_ready, i + 1)
                        nc.vector.tensor_copy(m_sb[:, 2 * i:2 * i + 2, :],
                                              bank_ff[:, i % 2, :].rearrange("p (j n) -> p j n", j=2)).then_inc(m_copied, 1)
                if f == 0 and k == 2:
                    dve.wait_ge(in_sems["w2"], 16)
                    nc.vector.tensor_reduce(wabs[:, 1:2], w2_sb[:, :, :], AX.XY, ALU.add,
                                            apply_absolute_value=True).then_inc(wabs_ready, 1)
                if f == 0 and k == 3:
                    dve.wait_ge(wtot_ready, 1)
                    link(nc.vector.tensor_scalar(wmean[:, :], bank_ff[:, 1, 0:2], 1.0 / (INNER * D), 1e-5, ALU.mult, ALU.max))
                    link(nc.vector.reciprocal(winv[:, :], wmean[:, :]))
                    ternary(0, w1_sb[:, :, :].rearrange("p c n -> p (c n)"), w1q)
                if f == 1 and k == 0:
                    ternary(1, w2_sb[:, :, :].rearrange("p c n -> p (c n)"), w2q)

            def ternary(i, src, dst):
                link(nc.vector.tensor_scalar(src, src, winv[:, i:i + 1], 1.0, ALU.mult, ALU.min))
                link(nc.vector.tensor_scalar(src, src, -1.0, MAGIC, ALU.max, ALU.add))
                nc.vector.tensor_scalar(dst[:, :], src, MAGIC, None, ALU.subtract).then_inc(wq_ready, 1)

            def quantise(src, small, layer, root, count, deq, ready):
                nc.vector.tensor_reduce(small(AMAX), src, AX.X, ALU.max, apply_absolute_value=True).then_inc(dve_link, 1)
                links["n"] += 1
                dve.wait_ge(root, count)
                dve.wait_ge(dve_link, links["base"] + links["n"])
                link(nc.vector.tensor_scalar(small(YMAX), small(AMAX), small(RRMS), 1e-5, ALU.mult, ALU.max))
                nc.vector.tensor_scalar(deq, small(YMAX), 1.0 / QMAX, wmean[:, layer:layer + 1], ALU.mult, ALU.mult)
                link(nc.vector.reciprocal(small(YINV), small(YMAX)))
                link(nc.vector.tensor_scalar(small(QMUL), small(YINV), QMAX, small(RRMS), ALU.mult, ALU.mult))
                nc.vector.tensor_scalar(src, src, small(QMUL), MAGIC, ALU.mult, ALU.add).then_inc(ready, 1)

            def take_wait():
                nc.vector.memset(pad[:, :], 0.0)

            def layer_norm_h(f):
                if True:
                    dve.wait_ge(h_rstd, f - 2)
                    link(nc.vector.scalar_tensor_tensor(h[:, :], z[:, :], h_mv[:, 0:1], g_bc[:, :], ALU.subtract, ALU.mult))
                    nc.vector.scalar_tensor_tensor(h[:, :], h[:, :], hs(RSTD), lb_bc[:, :], ALU.mult, ALU.add).then_inc(h_ready, 1)
                pass

            def feed_forward_first(f, k):
                if k == 1 and there(f, 2):
                    dve.wait_ge(up_ready, f - 1)
                    for half in range(2):
                        last = nc.vector.scalar_tensor_tensor(z[:, half * 512:(half + 1) * 512], bank_ff[:, half, :],
                                                              x_deq[:, 0:1], b1_bc[:, half * 512:(half + 1) * 512],
                                                              ALU.mult, ALU.add)
                    last.then_inc(z_done, 1)

            def feed_forward(f, k):
                if k == 0 and there(f, 3):
                    layer_norm_h(f)
                if k == 1 and there(f, 3):
                    dve.wait_ge(h_ready, f - 2)
                    quantise(h[:, :], hs, 1, h_rrms, f - 2, h_deq[:, 0:1], hq_ready)
                if k == 2 and there(f, 1):
                    x1 = x_all[:, f - 1, :]
                    dve.wait_ge(attn_ready, f)
                    nc.vector.scalar_tensor_tensor(x1, bank_ff[:, 0, 0:D], tgate[:, 0:1], x1, ALU.mult, ALU.add).then_inc(x1_done, 1)
                    dve.wait_ge(x1_done, f)
                    take_wait()
                    link(nc.vector.bn_stats(x_stats[:, :], x1))
                    take_wait()
                    nc.vector.bn_aggr(x_mv[:, :], x_stats[:, :]).then_inc(x_moments, 1)
                    dve.wait_ge(x_rstd, f)
                    link(nc.vector.tensor_scalar(xl[:, :], x1, x_mv[:, 0:1], xs(RSTD), ALU.subtract, ALU.mult))
                    quantise(xl[:, :], xs, 0, x_rrms, f, x_deq[:, 0:1], xq_ready)
                if k == 3 and there(f, 2):
                    dve.wait_ge(gelu_done, f - 1)
                    for i in range(2):
                        last = nc.vector.bn_stats(h_stats[:, 6 * i:6 * i + 6], z[:, 512 * i:512 * i + 512])
                    link(last)
                    take_wait()
                    nc.vector.bn_aggr(h_mv[:, :], h_stats[:, :]).then_inc(h_moments, 1)
                if k == 3 and there(f, 3):
                    dve.wait_ge(down_ready, f - 2)
                    link(nc.vector.scalar_tensor_tensor(ytmp[:, :], bank_ff[:, 0, 0:D], h_deq[:, 0:1], b2_bc[:, :],
                                                        ALU.mult, ALU.add))
                    if not (known(f) and f == 3):
                        dve.wait_ge(out_stored, 16 * (f - 3))
                    nc.vector.scalar_tensor_tensor(y[:, :], ytmp[:, :], tgate[:, 1:2], x_all[:, f - 3, :],
                                                   ALU.mult, ALU.add).then_inc(y_done, 1)

            def softmax_max(f, k, kts):
                n = step_no(f, k)
                dve.wait_ge(score_ready, n + 1)
                if not (known(n) and n < 2):
                    dve.wait_ge(exp_done, n - 1)
                nc.vector.tensor_reduce(neg_max[:, k % 2, :], score_banks(k, kts), AX.X, ALU.max,
                                        negate=True).then_inc(max_done, 1)

            def normalise(f, k):
                n = step_no(f, k)
                dve.wait_ge(lat_ready, n + 1)
                src = bank_lat[:, 0:GROUP * (KVC + 1)].rearrange("p (h c) -> p h c", h=GROUP)
                nc.vector.reciprocal(rsum[:, k % 2, :], src[:, :, KVC]).then_inc(rsum_done, 1)
                if not (known(n) and n < 2):
                    dve.wait_ge(latT_ready, n - 1)
                dve.wait_ge(rsum_done, n + 1)
                nc.vector.tensor_tensor(lat[:, k % 2, :, :], src[:, :, 0:KVC],
                                        rsum[:, k % 2, :].unsqueeze(2).broadcast_to([P, GROUP, KVC]),
                                        ALU.mult).then_inc(lat_done, 1)

            dve.wait_ge(gates_done, 1)
            for name in ("b1", "b2", "g", "lb"):
                dve.wait_ge(in_sems[name], 16)
            LINKS = 13
            so_far = links["n"]

            def main(kts):
                links["base"], links["n"] = so_far, 0

                def before(f):
                    if f is None:
                        links["start"] = links["base"] + links["n"]
                    elif not known(f):
                        links["base"], links["n"] = links["start"] + (f - LEAD) * LINKS, 0
                    elif f == F - 1:
                        links["base"], links["n"] = links["start"] + (F - 1 - LEAD) * LINKS, 0

                def body(f):
                    for k in range(STEPS):
                        n = step_no(f, k)
                        feed_forward_first(f, k)
                        if not known(f) or f < F:
                            softmax_max(f, k, kts)
                        if not known(f) or n + AHEAD < N:
                            turn_step(*ahead(f, k))
                        if not known(f) or 1 <= n < N + 1:
                            normalise(*behind(f, k, 1))
                        prepare(f, k)
                        feed_forward(f, k)
                    assert known(f) or links["n"] == LINKS, links["n"]

                run_tiles(dve, body, before)

            choose(dve, main)


_INS = ['x', 'ctx_2048', 'itok_BxS_0_1023', 'g_xattn', 'g_ffn', 'L0_xattn_W_kvc', 'L0_xattn_W_dq',
        'L0_xattn_W_uq', 'L0_xattn_W_qr', 'L0_xattn_W_uk', 'L0_xattn_W_kr', 'L0_xattn_W_uv', 'L0_xattn_W_o',
        'L0_ffn_w1', 'L0_ffn_b1', 'L0_ffn_ln_g', 'L0_ffn_ln_b', 'L0_ffn_w2', 'L0_ffn_b2']


def kernel(**inputs):
    import numpy as _np
    import concourse.bacc as _bacc
    from concourse import mybir as _mybir
    from concourse.bass_utils import run_bass_kernel_spmd as _run

    nc = _bacc.Bacc("TRN2", target_bir_lowering=False, num_devices=1)
    arrays, args = {}, []
    for name in _INS:
        a = _np.ascontiguousarray(inputs[name])
        arrays[f"in_{name}"] = a
        args.append(nc.dram_tensor(f"in_{name}", a.shape, _mybir.dt.from_np(a.dtype), kind="ExternalInput").ap())
    c = shape_constants()
    arrays["in_consts"] = c
    args.append(nc.dram_tensor("in_consts", c.shape, _mybir.dt.from_np(c.dtype), kind="ExternalInput").ap())
    args.append(nc.dram_tensor("out_x", (B, S, D), _mybir.dt.float32, kind="ExternalOutput").ap())
    build(nc, *args)
    r = _run(nc, [arrays], core_ids=[0])
    return r.results[0]["out_x"]
```

```python
from contextlib import ExitStack

import numpy as np
import concourse.bass as bass
from concourse import mybir

B, S, D = 4, 256, 256
H, HD, R = 16, 128, 64
KVC, QC = 64, 96
INNER = 1024
LOOKBACK = 8
P = 128
TILES = S // P
DC = D // P
IC = INNER // P
PAIRS = H // 2
GROUP = 4
STEPS = H // GROUP
F = B * TILES
N = F * STEPS
AHEAD = 2
SCALE = float(1.0 / np.sqrt(np.float32(HD + R)))
NEG = -1e30
EPS = 1e-5
MAGIC = 12582912.0
QMAX = 127.0
EYE, IOTA, COS, SIN, CONSTS = 0, P, P + S, P + 3 * S, P + 4 * S


def shape_constants():
    half = R // 2
    freq = (np.float32(1.0) / np.float32(10000.0) ** (np.arange(half, dtype=np.float32) / np.float32(half)))
    ang = np.arange(S, dtype=np.float32)[None, :] * freq.astype(np.float32)[:, None]
    cos, sin = np.cos(ang).astype(np.float32), np.sin(ang).astype(np.float32)
    one = np.ones((KVC, S), np.float32)
    c = np.zeros((P, CONSTS), np.float32)
    c[:, EYE:EYE + P] = np.eye(P, dtype=np.float32)
    c[:, IOTA:IOTA + S] = np.arange(S, dtype=np.float32)[None, :] + LOOKBACK / 2
    c[:, COS:COS + S] = np.concatenate([one, cos, cos])
    c[:, COS + S:COS + 2 * S] = np.concatenate([cos, cos, one])
    c[:, SIN:SIN + S] = np.concatenate([-sin, sin, -sin, sin])
    return c


def build(nc, x, ctx_kv, itok, g_xattn, g_ffn, W_kvc, W_dq, W_uq, W_qr, W_uk, W_kr, W_uv, W_o,
          w1, b1, ln_g, ln_b, w2, b2, consts, out):
    fp32, bf16, i32 = mybir.dt.float32, mybir.dt.bfloat16, mybir.dt.int32
    ALU, ACT, AX = mybir.AluOpType, mybir.ActivationFunctionType, mybir.AxisListType
    KT = S // P

    with ExitStack() as stack:
        def sb(name, shape, dt=fp32):
            return stack.enter_context(nc.sbuf_tensor(name, shape, dt))

        def ps(name, shape, dt=fp32):
            return stack.enter_context(nc.psum_tensor(name, shape, dt))

        def sem(name):
            return stack.enter_context(nc.semaphore(name))

        x_all = sb("x_all", [P, F, D])
        ctx_all = sb("ctx_all", [P, F, D])
        seg_i = sb("seg_i", [P, F], i32)
        cst = sb("cst", [P, CONSTS])
        wdq = sb("wdq", [P, DC, QC])
        wkvc = sb("wkvc", [P, DC, 2, KVC])
        wkr = sb("wkr", [KVC, 2, R])
        wuq = sb("wuq", [QC, H, HD])
        wuk_wuv = sb("wuk_wuv", [P, H, HD])
        wo = sb("wo", [HD, H, D])
        w1_sb = sb("w1_sb", [P, IC, D])
        w2_sb = sb("w2_sb", [P, DC, INNER])
        b1_bc = sb("b1_bc", [P, INNER])
        g_bc = sb("g_bc", [P, INNER])
        lb_bc = sb("lb_bc", [P, INNER])
        b2_bc = sb("b2_bc", [P, D])
        gates = sb("gates", [P, 2])
        wuk = wuk_wuv[0:KVC, :, :]

        wuqT = sb("wuqT", [HD, 2, 4, QC])
        wukT = sb("wukT", [HD, 2, 4, KVC])
        wcat = sb("wcat", [QC, PAIRS, 2, P])
        wswap = sb("wswap", [QC, PAIRS, P])
        wkr_swap = sb("wkr_swap", [KVC, 2, R])
        m_sb = sb("m_sb", [P, PAIRS, D])
        w1T = sb("w1T", [P, DC, INNER], bf16)
        w2T = sb("w2T", [P, IC, D], bf16)
        w1q = sb("w1q", [P, IC * D], bf16)
        w2q = sb("w2q", [P, DC * INNER], bf16)

        eye_b = sb("eye_b", [P, P], bf16)
        ones = sb("ones", [P, P])
        half_neg = sb("half_neg", [P, F])
        eps = sb("eps", [P, F])
        pad = sb("pad", [P, 2])
        mask = sb("mask", [P, F, S], bf16)
        seg_f = sb("seg_f", [P, F])
        neg_seg = sb("neg_seg", [P, F])
        far = sb("far", [P, F])
        farthest = sb("farthest", [P, 2])
        wide = sb("wide", [1, 1], i32)
        tgate = sb("tgate", [P, 2])
        wabs = sb("wabs", [P, 2])
        wmean = sb("wmean", [P, 2])
        winv = sb("winv", [P, 2])

        prob_room = sb("prob_room", [P, 2 * GROUP * KT * P])
        xnT, ctxT = (prob_room[:, o:o + 2 * DC * S].rearrange("p (n c s) -> p n c s", n=2, c=DC) for o in (0, 2 * DC * S))
        probT_room = sb("probT_room", [P, 2 * KT * GROUP * P])
        xn = probT_room[:, :].rearrange("p (f n) -> p f n", f=F)
        a_stats = sb("a_stats", [P, F, 6])
        a_mv = sb("a_mv", [P, F, 2])
        a_var = sb("a_var", [P, F])
        a_root = sb("a_root", [P, F])
        qcT = sb("qcT", [QC, B * S])
        kcat = sb("kcat", [P, B, 2, S])
        kvc1 = sb("kvc1", [P, B * KT, KVC + 1])

        qcat = sb("qcat", [P, STEPS, 2, 2, P])
        turned = sb("turned", [P, 2, S])
        prob = prob_room[:, :].rearrange("p (n h s) -> p n h s", n=2, h=GROUP)
        probT = probT_room[:, :].rearrange("p (n t h s) -> p n t h s", n=2, t=KT, h=GROUP)
        neg_max = sb("neg_max", [P, 2, GROUP])
        rsum = sb("rsum", [P, 2, GROUP])
        lat = sb("lat", [P, 2, GROUP, KVC])
        latT = sb("latT", [P, PAIRS, P])

        x_stats = sb("x_stats", [P, 6])
        x_mv = sb("x_mv", [P, 2])
        x_small = sb("x_small", [P, 9])
        xl = sb("xl", [P, D])
        xqT = sb("xqT", [P, DC, P], bf16)
        z = sb("z", [P, 2, INNER])
        tanh_z = sb("tanh_z", [P, INNER])
        h_stats = sb("h_stats", [P, 12])
        h_mv = sb("h_mv", [P, 2])
        h_small = sb("h_small", [P, 9])
        h = sb("h", [P, 2, INNER])
        wuvT = h[:, 1, :].rearrange("p (h c) -> p h c", h=H)
        hqT = sb("hqT", [P, IC, P], bf16)
        junk = sb("junk", [P, INNER], bf16)
        ytmp = sb("ytmp", [P, D])
        y = sb("y", [P, D])
        VAR, RSTD, SQ, MS, RRMS, AMAX, YMAX, YINV, QMUL = range(9)
        halves = [slice(i * INNER // 2, (i + 1) * INNER // 2) for i in range(2)]
        x_deq = sb("x_deq", [P, 1])
        h_deq = sb("h_deq", [P, 1])

        def xs(i):
            return x_small[:, i:i + 1]

        def hs(i):
            return h_small[:, i:i + 1]

        bank_pair = ps("bank_pair", [P, 512])
        bank_swap = ps("bank_swap", [P, 512])
        bank_score = ps("bank_score", [P, 2, 512])
        bank_prob = ps("bank_prob", [P, 512])
        bank_lat = ps("bank_lat", [P, 512])
        bank_ff = ps("bank_ff", [P, 2, 512])

        in_sems = {n: sem("in_" + n) for n in (
            "x0", "x1", "x2", "ctx0", "ctx1", "ctx2", "seg", "eye", "rope", "wdq", "wkvc", "wkr", "wuq", "wqr0", "wqr1", "wuk", "wuv",
            "wo", "w1", "w2", "b1", "g", "lb", "b2", "gate0", "gate1")}
        out_stored = sem("out_stored")
        consts_made = sem("consts_made")
        mask_made = sem("mask_made")
        far_ready = sem("far_ready")
        far_turned = sem("far_turned")
        wide_ready = sem("wide_ready")
        kweights = sem("kweights")
        wcopies = sem("wcopies")
        seg_ready = sem("seg_ready")
        dist_ready = sem("dist_ready")
        gates_done = sem("gates_done")
        a_var_ready = sem("a_var_ready")
        a_root_ready = sem("a_root_ready")
        xn_ready = sem("xn_ready")
        xT_ready = sem("xT_ready")
        xT_copied = sem("xT_copied")
        cT_ready = sem("cT_ready")
        cT_copied = sem("cT_copied")
        qc_ready = sem("qc_ready")
        qc_copied = sem("qc_copied")
        kvc_ready = sem("kvc_ready")
        kvc_copied = sem("kvc_copied")
        kvk_ready = sem("kvk_ready")
        kvk_copied = sem("kvk_copied")
        wt_ready = sem("wt_ready")
        wt_copied = sem("wt_copied")
        fold_ready = sem("fold_ready")
        fold_copied = sem("fold_copied")
        wuvT_ready = sem("wuvT_ready")
        wuvT_copied = sem("wuvT_copied")
        m_ready = sem("m_ready")
        m_copied = sem("m_copied")
        wabs_ready = sem("wabs_ready")
        wtot_ready = sem("wtot_ready")
        wq_ready = sem("wq_ready")
        wqT_ready = sem("wqT_ready")
        wqT_copied = sem("wqT_copied")
        pair_ready = sem("pair_ready")
        pair_turned = sem("pair_turned")
        pair_half = sem("pair_half")
        pair_done = sem("pair_done")
        score_ready = sem("score_ready")
        max_done = sem("max_done")
        exp_done = sem("exp_done")
        probT_ready = sem("probT_ready")
        probT_copied = sem("probT_copied")
        lat_ready = sem("lat_ready")
        rsum_done = sem("rsum_done")
        lat_done = sem("lat_done")
        latT_ready = sem("latT_ready")
        latT_copied = sem("latT_copied")
        attn_ready = sem("attn_ready")
        x1_done = sem("x1_done")
        x_moments = sem("x_moments")
        x_root = sem("x_root")
        xq_ready = sem("xq_ready")
        xqT_ready = sem("xqT_ready")
        xqT_copied = sem("xqT_copied")
        up_ready = sem("up_ready")
        z_done = sem("z_done")
        tanh_done = sem("tanh_done")
        silu_done = sem("silu_done")
        gelu_done = sem("gelu_done")
        h_moments = sem("h_moments")
        h_rstd = sem("h_rstd")
        h_ready = sem("h_ready")
        h_sumsq = sem("h_sumsq")
        h_rrms = sem("h_rrms")
        hq_ready = sem("hq_ready")
        hqT_ready = sem("hqT_ready")
        hqT_copied = sem("hqT_copied")
        down_ready = sem("down_ready")
        y_done = sem("y_done")
        dve_link = sem("dve_link")
        pool_link = sem("pool_link")

        eye = cst[:, EYE:EYE + P]
        iota = cst[:, IOTA:IOTA + S]
        cos_tab = cst[:, COS:COS + 2 * S].rearrange("p (e s) -> p e s", e=2)
        sin_tab = cst[:, SIN:SIN + S]

        def known(v):
            return isinstance(v, int)

        def behind(f, k, d):
            return (f, k - d) if k >= d else (f - 1, k - d + STEPS)

        def ahead(f, k):
            return (f, k + AHEAD) if k + AHEAD < STEPS else (f + 1, k + AHEAD - STEPS)

        def step_no(f, k):
            return f * STEPS + k

        def choose(eng, main):
            eng.wait_ge(wide_ready, 1)
            w = eng.value_load(wide[0:1, 0:1], min_val=0, max_val=1)
            with eng.If(w == 0):
                main(1)
            with eng.Else():
                main(KT)

        LEAD = 3

        def run_tiles(eng, body, after, before=lambda f: None):
            for f in range(LEAD):
                before(f)
                body(f)
            before(None)
            with eng.Fori(LEAD, F - 1) as f:
                before(f)
                body(f)
            before(F - 1)
            body(F - 1)
            after()

        def slot(c):
            return 1 if known(c) and c == F - 2 else 0

        def last_tile(c):
            return known(c) and c == F - 1

        def down_bank(c):
            return bank_pair[:, 0:D] if last_tile(c) else bank_ff[:, 0, 0:D]

        def there(f, lag):
            return not known(f) or 0 <= f - lag < F

        def score_banks(k, kts):
            banks = bank_score[:, k % 2, :] if kts == 1 else bank_score[:, :, :].rearrange("p i s -> p (i s)")
            return banks.rearrange("p (h s) -> p h s", h=GROUP)

        groups = ((0, TILES), (TILES, 2 * TILES), (2 * TILES, F))

        def load_group(load, dst, src, i, name):
            lo, hi = groups[i]
            load(dst[:, lo:hi, :], src[:, lo:hi, :], f"{name}{i}")

        def input_banks(b):
            return bank_score if b % 2 == 0 else bank_ff

        def fold_bank(i):
            return bank_prob if i % 2 == 0 else bank_lat

        def square_dist(i):
            return z[:, i // (F // 2), i % (F // 2) * S:(i % (F // 2) + 1) * S]

        block = stack.enter_context(nc.Block())

        @block.sync
        def _(sp):
            def load(dst, src, name):
                sp.dma_start(dst, src).then_inc(in_sems[name], 16)

            x_v = x.rearrange("b (t p) d -> p (b t) d", p=P)
            load(cst[:, EYE:IOTA], consts[:, EYE:IOTA], "eye")
            load_group(load, x_all, x_v, 0, "x")
            load(wdq[:, :, :], W_dq.rearrange("(c p) n -> p c n", p=P), "wdq")
            load_group(load, x_all, x_v, 1, "x")
            load(cst[:, IOTA:CONSTS], consts[:, IOTA:CONSTS], "rope")
            with nc.allow_non_contiguous_dma(reason="1024 token numbers"):
                load(seg_i[:, :], itok.rearrange("b (t p) -> p (b t)", p=P), "seg")
            load_group(load, x_all, x_v, 2, "x")
            load_group(load, ctx_all, ctx_kv.rearrange("b (t p) d -> p (b t) d", p=P), 2, "ctx")
            wqr_pair = W_qr.rearrange("k (j e n) -> k j e n", e=2, n=R)
            load(wcat[:, :, 0, KVC:P], wqr_pair[:, :, 0, :], "wqr0")
            load(wcat[:, :, 1, 0:R], wqr_pair[:, :, 1, :], "wqr1")
            load(wuq[:, :, :], W_uq.rearrange("k (h n) -> k h n", h=H), "wuq")
            load(wuk, W_uk.rearrange("k (h n) -> k h n", h=H), "wuk")
            load(wuk_wuv[KVC:P, :, :], W_uv.rearrange("k (h n) -> k h n", h=H), "wuv")
            load(wo[:, :, :], W_o.rearrange("(h p) n -> p h n", p=P), "wo")
            load(gates[:, 0:1], g_xattn.partition_broadcast(P), "gate0")
            load(gates[:, 1:2], g_ffn.partition_broadcast(P), "gate1")
            load(w1_sb[:, :, :], w1.rearrange("(c p) n -> p c n", p=P), "w1")
            load(w2_sb[:, :, :], w2.rearrange("(c p) n -> p c n", p=P), "w2")
            load(b1_bc[:, :], b1.partition_broadcast(P), "b1")
            load(g_bc[:, :], ln_g.partition_broadcast(P), "g")
            load(lb_bc[:, :], ln_b.partition_broadcast(P), "lb")
            load(b2_bc[:, :], b2.partition_broadcast(P), "b2")

            out_v = out.rearrange("b (t p) d -> (b t) p d", p=P)
            with sp.Fori(0, F) as f:
                sp.wait_ge(y_done, f + 1)
                sp.dma_start(out_v[bass.ds(f, 1), :, :].rearrange("o p d -> p (o d)"), y[:, :]).then_inc(out_stored, 16)
            sp.wait_ge(out_stored, 16 * F)

        @block.gpsimd
        def _(pool):
            half = R // 2
            pool.wait_ge(consts_made, 1)

            def input_root(b):
                lo, hi = b * TILES, (b + 1) * TILES
                pool.wait_ge(a_var_ready, b + 1)
                nc.gpsimd.tensor_tensor(a_root[:, lo:hi], a_var[:, lo:hi], half_neg[:, lo:hi], ALU.pow).then_inc(a_root_ready, 1)

            input_root(0)
            pool.wait_ge(in_sems["wkvc"], 16)
            nc.gpsimd.tensor_copy(wkvc[:, :, 1, :], wkvc[:, :, 0, :]).then_inc(kweights, 1)
            pool.wait_ge(in_sems["wkr"], 16)
            for e in range(2):
                nc.gpsimd.tensor_copy(wkr_swap[:, e, 0:half], wkr[:, 0, half:R])
                nc.gpsimd.tensor_copy(wkr_swap[:, e, half:R], wkr[:, 0, 0:half])
            nc.gpsimd.tensor_copy(wkr[:, 1, :], wkr[:, 0, :]).then_inc(kweights, 1)
            for b in range(1, B):
                input_root(b)

            def add_rope(even, odd, add_even, add_odd, s):
                pool.wait_ge(pair_turned, s + 1)
                nc.gpsimd.tensor_tensor(odd, odd, add_odd, ALU.add).then_inc(pair_half, 1)
                pool.wait_ge(pair_half, s + 1)
                nc.gpsimd.tensor_tensor(even, even, add_even, ALU.add).then_inc(pair_done, 1)
                pool.wait_ge(pair_done, s + 1)

            with pool.Fori(0, B // 2) as i:
                for e in range(2):
                    b = 2 * i + e
                    add_rope(kcat[KVC:P, b, 0, :], kcat[0:R, b, 1, :], turned[KVC:P, e, :], turned[0:R, e, :], b)

            def add_rope_step(f, k):
                t = turned[:, k % 2, :].rearrange("p (j s) -> p j s", j=2)
                add_rope(qcat[KVC:P, k, :, 0, :], qcat[0:R, k, :, 1, :], t[KVC:P, :, :], t[0:R, :, :], B + step_no(f, k))

            for k in range(AHEAD):
                add_rope_step(0, k)

            links = {"base": 0, "n": 0}

            def link(ins):
                links["n"] += 1
                ins.then_inc(pool_link, 1)
                pool.wait_ge(pool_link, links["base"] + links["n"])

            def small(dst, a, b, op):
                return nc.gpsimd.tensor_tensor(dst, a, b, op)

            pow_half, eps1 = half_neg[:, 0:1], eps[:, 0:1]

            def root_hq(c):
                pool.wait_ge(h_sumsq, c + 1)
                link(small(hs(MS), hs(SQ), eps1, ALU.add))
                small(hs(RRMS), hs(MS), pow_half, ALU.pow).then_inc(h_rrms, 1)

            def root_x(c):
                pool.wait_ge(x_moments, c + 1)
                small(xs(RRMS), xs(MS), pow_half, ALU.pow).then_inc(x_root, 1)

            def root_h(c):
                pool.wait_ge(h_moments, c + 1)
                link(small(hs(VAR), h_mv[:, 1:2], eps1, ALU.add))
                small(hs(RSTD), hs(VAR), pow_half, ALU.pow).then_inc(h_rstd, 1)

            def feed_forward(f, k):
                if k == 1 and there(f, 3):
                    root_hq(f - 3)
                if k == 2 and there(f, 1):
                    root_x(f - 1)
                if k == 3 and there(f, 2):
                    root_h(f - 2)

            LINKS = 2

            def before(f):
                if f is None:
                    links["start"] = links["base"] + links["n"]
                    return
                if known(f):
                    if f == F - 1:
                        links["base"], links["n"] = links["start"] + (F - 1 - LEAD) * LINKS, 0
                else:
                    links["base"], links["n"] = links["start"] + (f - LEAD) * LINKS, 0

            def body(f):
                for k in range(STEPS):
                    if not known(f) or step_no(f, k) + AHEAD < N:
                        add_rope_step(*ahead(f, k))
                    feed_forward(f, k)
                assert known(f) or links["n"] == LINKS, links["n"]

            def after():
                root_x(F - 1)
                root_h(F - 2)
                root_hq(F - 3)
                root_h(F - 1)
                root_hq(F - 2)
                root_hq(F - 1)

            run_tiles(pool, body, after, before)

        @block.scalar
        def _(act):
            def load(dst, src, name):
                act.dma_start(dst, src).then_inc(in_sems[name], 16)

            ctx_v = ctx_kv.rearrange("b (t p) d -> p (b t) d", p=P)
            load_group(load, ctx_all, ctx_v, 0, "ctx")
            load(wkvc[:, :, 0, :], W_kvc.rearrange("(c p) n -> p c n", p=P), "wkvc")
            load(wkr[:, 0, :], W_kr, "wkr")
            load_group(load, ctx_all, ctx_v, 1, "ctx")

            def copy_x(b):
                act.wait_ge(xT_ready, b + 1)
                if b >= 2:
                    act.wait_ge(qc_ready, b - 1)
                nc.scalar.copy(xnT[:, b % 2, :, :], input_banks(b)[:, 0, :].rearrange("p (c s) -> p c s", c=DC)).then_inc(xT_copied, 1)

            def copy_latents(b):
                act.wait_ge(kvc_ready, b + 1)
                nc.scalar.copy(kcat[0:KVC, b, 0, :], bank_lat[0:KVC, 0:S])
                nc.scalar.copy(kcat[KVC:P, b, 1, :], bank_lat[KVC:P, 0:S]).then_inc(kvc_copied, 1)
                act.wait_ge(qc_ready, b + 1)
                nc.scalar.activation(qcT[:, b * S:(b + 1) * S], bank_prob[0:QC, 0:S], ACT.Copy,
                                     scale=SCALE).then_inc(qc_copied, 1)

            def copy_keys(b):
                act.wait_ge(kvk_ready, b + 1)
                nc.scalar.copy(kvc1[:, b * KT:(b + 1) * KT, 0:KVC],
                               bank_prob[:, S:S + KT * KVC].rearrange("p (t c) -> p t c", t=KT)).then_inc(kvk_copied, 1)

            def square_dists(b):
                for i in range(b * TILES, (b + 1) * TILES):
                    last = nc.scalar.activation(square_dist(i), iota, ACT.Square, bias=neg_seg[:, i:i + 1])
                last.then_inc(dist_ready, 1)

            act.wait_ge(consts_made, 1)
            nc.scalar.activation(tgate[:, 0:1], eps[:, 0:1], ACT.Exp)
            copy_x(0)
            copy_latents(0)
            for b in range(1, B):
                copy_x(b)
                copy_keys(b - 1)
                if b == 1:
                    act.wait_ge(seg_ready, 1)
                    act.wait_ge(in_sems["rope"], 16)
                square_dists(b - 1)
                copy_latents(b)
            copy_keys(B - 1)
            square_dists(B - 1)

            for i in range(H // 4):
                act.wait_ge(wt_ready, i + 1)
                if i >= 2:
                    act.wait_ge(fold_ready, i - 1)
                nc.scalar.copy(wuqT[:, i % 2, :, :], input_banks(i)[:, 0, 0:4 * QC].rearrange("p (h c) -> p h c", h=4))
                nc.scalar.copy(wukT[:, i % 2, :, :],
                               input_banks(i)[:, 1, 0:4 * KVC].rearrange("p (h c) -> p h c", h=4)).then_inc(wt_copied, 1)

            for k in range(H // 8):
                act.wait_ge(wuvT_ready, k + 1)
                nc.scalar.copy(wuvT[:, 8 * k:8 * k + 8, :],
                               bank_ff[:, k, :].rearrange("p (h c) -> p h c", h=8)).then_inc(wuvT_copied, 1)

            act.wait_ge(in_sems["gate0"], 16)
            act.wait_ge(in_sems["gate1"], 16)
            nc.scalar.activation(tgate[:, :], gates[:, :], ACT.Tanh).then_inc(gates_done, 1)

            def prepare(f, k):
                if known(f) and f == 0 and k < 2:
                    name, src, room = (("w1", w1_sb, w1q), ("w2", w2_sb, w2q))[k]
                    act.wait_ge(in_sems[name], 16)
                    nc.scalar.activation(room[:, :], src[:, :, :].rearrange("p c n -> p (c n)"), ACT.Abs,
                                         accum_out=wabs[:, k:k + 1]).then_inc(wabs_ready, 1)
                if known(f) and f == 1:
                    act.wait_ge(wqT_ready, k + 1)
                    src = bank_ff[:, 1, :].bitcast(bf16)
                    dst = w1T[:, k, :] if k < 2 else w2T[:, 4 * (k - 2):4 * (k - 1), :]
                    if k >= 2:
                        src = src.rearrange("p (c n) -> p c n", c=4)
                    nc.scalar.copy(dst, src).then_inc(wqT_copied, 1)

            def copy_x1(c):
                act.wait_ge(xqT_ready, c + 1)
                nc.scalar.activation(xqT[:, :, :], bank_ff[:, 1, 0:D].rearrange("p (c s) -> p c s", c=DC),
                                     ACT.Copy, bias=-MAGIC).then_inc(xqT_copied, 1)

            def tanh(c):
                for i, part in enumerate(halves):
                    act.wait_ge(z_done, 2 * c + i + 1)
                    nc.scalar.activation(tanh_z[:, part], z[:, slot(c), part], ACT.Tanh, scale=0.5).then_inc(tanh_done, 1)

            def gelu(c, scale=0.5):
                for i, part in enumerate(halves):
                    act.wait_ge(silu_done, 2 * c + i + 1)
                    nc.scalar.activation(z[:, slot(c), part], z[:, slot(c), part], ACT.Gelu, scale=scale).then_inc(gelu_done, 1)

            def silu(c):
                for i, part in enumerate(halves):
                    act.wait_ge(z_done, 2 * c + i + 1)
                    nc.scalar.activation(z[:, slot(c), part], z[:, slot(c), part], ACT.Silu).then_inc(silu_done, 1)

            def sum_squares(c):
                act.wait_ge(h_ready, c + 1)
                nc.scalar.activation(junk[:, :], h[:, slot(c), :], ACT.Square, scale=float(INNER) ** -0.5,
                                     accum_out=hs(SQ)).then_inc(h_sumsq, 1)

            def copy_h(c, r):
                act.wait_ge(hqT_ready, 2 * c + r + 1)
                nc.scalar.activation(hqT[:, 4 * r:4 * r + 4, :], bank_ff[:, 1 - r, :].rearrange("p (c s) -> p c s", c=4),
                                     ACT.Copy, bias=-MAGIC).then_inc(hqT_copied, 1)

            def copy_latT(f, k):
                n = step_no(f, k)
                act.wait_ge(latT_ready, n + 1)
                if not (known(f) and f == 0):
                    act.wait_ge(attn_ready, f)
                nc.scalar.copy(latT[:, 2 * k:2 * k + 2, :],
                               bank_lat[:, 0:2 * P].rearrange("p (j s) -> p j s", j=2)).then_inc(latT_copied, 1)

            def copy_probT(f, k, kts):
                n = step_no(f, k)
                if not (known(n) and n < 2):
                    act.wait_ge(lat_ready, n - 1)
                for kt in range(kts):
                    act.wait_ge(probT_ready, n * kts + kt + 1)
                    nc.scalar.copy(probT[:, k % 2, kt, :, :],
                                   bank_prob[:, :].rearrange("p (h s) -> p h s", h=GROUP)).then_inc(probT_copied, 1)

            def exponentials(f, k, kts):
                n = step_no(f, k)
                src = score_banks(k, kts)
                act.wait_ge(max_done, n + 1)
                if not (known(n) and n < 2):
                    act.wait_ge(probT_ready, (n - 1) * kts)
                for j in range(GROUP):
                    last = nc.scalar.activation(prob[:, k % 2, j, 0:kts * P], src[:, j, :], ACT.Exp,
                                                bias=neg_max[:, k % 2, j:j + 1])
                last.then_inc(exp_done, 1)

            def main(kts):
                def body(f):
                    for k in range(STEPS):
                        if not known(f) or step_no(f, k) >= 2:
                            copy_latT(*behind(f, k, 2))
                        if not known(f) or step_no(f, k) >= 1:
                            copy_probT(*behind(f, k, 1), kts)
                        if k == 0 and there(f, 2):
                            copy_x1(f - 2)
                        if k == 3 and there(f, 3):
                            copy_h(f - 3, 1)
                        if k == 1 and there(f, 3):
                            sum_squares(f - 3)
                        exponentials(f, k, kts)
                        prepare(f, k)
                        if k == 1 and there(f, 2):
                            tanh(f - 2)
                        if k == 2 and there(f, 3):
                            copy_h(f - 3, 0)
                        if k == 2 and there(f, 2):
                            gelu(f - 2)

                def after():
                    copy_latT(F - 1, STEPS - 2)
                    copy_x1(F - 2)
                    copy_probT(F - 1, STEPS - 1, kts)
                    silu(F - 2)
                    copy_latT(F - 1, STEPS - 1)
                    gelu(F - 2, 1.0)
                    copy_x1(F - 1)
                    sum_squares(F - 3)
                    silu(F - 1)
                    gelu(F - 1, 1.0)
                    for r in range(2):
                        copy_h(F - 3, r)
                    sum_squares(F - 2)
                    for r in range(2):
                        copy_h(F - 2, r)
                    sum_squares(F - 1)
                    for r in range(2):
                        copy_h(F - 1, r)

                run_tiles(act, body, after)

            choose(act, main)

        @block.tensor
        def _(pe):
            pe.wait_ge(in_sems["eye"], 16)

            def transpose_inputs(b):
                banks = input_banks(b)
                pe.wait_ge(in_sems[f"ctx{min(b, 2)}"], 16)
                if b >= 2:
                    pe.wait_ge(cT_copied, b - 1)
                for t in range(TILES):
                    for c in range(DC):
                        last = nc.tensor.transpose(banks[:, 1, c * S + t * P:c * S + (t + 1) * P],
                                                   ctx_all[:, b * TILES + t, c * P:(c + 1) * P], eye)
                last.then_inc(cT_ready, 1)
                pe.wait_ge(xn_ready, b + 1)
                if b >= 2:
                    pe.wait_ge(xT_copied, b - 1)
                for t in range(TILES):
                    for c in range(DC):
                        last = nc.tensor.transpose(banks[:, 0, c * S + t * P:c * S + (t + 1) * P],
                                                   xn[:, b * TILES + t, c * P:(c + 1) * P], eye)
                last.then_inc(xT_ready, 1)

            def latents(b):
                pe.wait_ge(cT_copied, b + 1)
                if b:
                    pe.wait_ge(kvc_copied, b)
                else:
                    pe.wait_ge(kweights, 1)
                    pe.wait_ge(in_sems["wdq"], 16)
                for c in range(DC):
                    last = nc.tensor.matmul(bank_lat[:, 0:S], wkvc[:, c, :, :].rearrange("p e n -> p (e n)"), ctxT[:, b % 2, c, :],
                                            start=(c == 0), stop=(c == DC - 1))
                last.then_inc(kvc_ready, 1)
                pe.wait_ge(xT_copied, b + 1)
                if b:
                    pe.wait_ge(kvk_copied, b)
                for c in range(DC):
                    last = nc.tensor.matmul(bank_prob[0:QC, 0:S], wdq[:, c, :], xnT[:, b % 2, c, :], start=(c == 0), stop=(c == DC - 1))
                last.then_inc(qc_ready, 1)

            def keys(b):
                pe.wait_ge(kvc_copied, b + 1)
                if b:
                    pe.wait_ge(pair_turned, b)
                else:
                    pe.wait_ge(kweights, 2)
                kvcT = kcat[0:KVC, b, 0, :]
                nc.tensor.matmul(bank_pair[:, 0:S], wkr[:, :, :].rearrange("k e n -> k (e n)"), kvcT, start=True, stop=True)
                nc.tensor.matmul(bank_swap[:, 0:S], wkr_swap[:, :, :].rearrange("k e n -> k (e n)"), kvcT,
                                 start=True, stop=True).then_inc(pair_ready, 1)
                pe.wait_ge(qc_copied, b + 1)
                for kt in range(KT):
                    last = nc.tensor.transpose(bank_prob[:, S + kt * KVC:S + (kt + 1) * KVC], kcat[0:KVC, b, 0, kt * P:(kt + 1) * P],
                                               eye[0:KVC, 0:KVC])
                last.then_inc(kvk_ready, 1)

            transpose_inputs(0)
            latents(0)
            for b in range(1, B):
                transpose_inputs(b)
                keys(b - 1)
                latents(b)
            keys(B - 1)

            pe.wait_ge(in_sems["wuq"], 16)
            pe.wait_ge(in_sems["wuk"], 16)
            pe.wait_ge(kvk_copied, B)

            def transpose_weights(i):
                banks = input_banks(i)
                if i >= 2:
                    pe.wait_ge(wt_copied, i - 1)
                for j in range(4):
                    nc.tensor.transpose(banks[:, 0, j * QC:(j + 1) * QC], wuq[:, 4 * i + j, :], eye[0:QC, 0:QC])
                    last = nc.tensor.transpose(banks[:, 1, j * KVC:(j + 1) * KVC], wuk[:, 4 * i + j, :], eye[0:KVC, 0:KVC])
                last.then_inc(wt_ready, 1)

            def fold(i):
                pe.wait_ge(wt_copied, i + 1)
                if i >= 2:
                    pe.wait_ge(fold_copied, i - 1)
                for j in range(4):
                    last = nc.tensor.matmul(fold_bank(i)[0:QC, j * KVC:(j + 1) * KVC], wuqT[:, i % 2, j, :], wukT[:, i % 2, j, :],
                                            start=True, stop=True)
                last.then_inc(fold_ready, 1)

            def project(f, k):
                s = B + step_no(f, k)
                pe.wait_ge(pair_turned, s)
                src = qcT[:, bass.ds(f * P, P)]
                for j in range(2):
                    for e in range(2):
                        nc.tensor.matmul(bank_pair[:, (2 * j + e) * P:(2 * j + e + 1) * P], wcat[:, 2 * k + j, e, :], src,
                                         start=True, stop=True)
                for j in range(2):
                    last = nc.tensor.matmul(bank_swap[:, j * P:(j + 1) * P], wswap[:, 2 * k + j, :], src, start=True, stop=True)
                last.then_inc(pair_ready, 1)

            transpose_weights(0)
            transpose_weights(1)
            fold(0)
            transpose_weights(2)
            fold(1)
            transpose_weights(3)
            pe.wait_ge(wcopies, 1)
            pe.wait_ge(fold_copied, 1)
            project(0, 0)
            fold(2)
            fold(3)
            pe.wait_ge(far_ready, 1)
            nc.tensor.matmul(bank_ff[0:1, 0, 0:P], farthest[:, 0:1], eye, start=True, stop=True).then_inc(far_turned, 1)
            pe.wait_ge(fold_copied, 2)
            project(0, 1)
            pe.wait_ge(in_sems["wuv"], 16)
            pe.wait_ge(wide_ready, 1)
            for i in range(H // 8):
                for j in range(8):
                    last = nc.tensor.transpose(bank_ff[:, i, j * KVC:(j + 1) * KVC], wuk_wuv[KVC:P, 8 * i + j, :],
                                               eye[KVC:P, KVC:P])
                last.then_inc(wuvT_ready, 1)
            pe.wait_ge(fold_copied, H // 4)

            def prepare_end(f, k):
                if known(f) and f == 0:
                    if k == 1:
                        pe.wait_ge(in_sems["wo"], 16)
                        pe.wait_ge(wuvT_copied, 2)
                    if k in (1, 2):
                        for i in (2 * k - 2, 2 * k - 1):
                            if i >= 2:
                                pe.wait_ge(m_copied, i - 1)
                            for j in range(4):
                                hh = 4 * i + j
                                last = nc.tensor.matmul(bank_ff[(j % 2) * KVC:(j % 2 + 1) * KVC, i % 2, (j // 2) * D:(j // 2 + 1) * D],
                                                        wuvT[:, hh, :], wo[:, hh, :], start=True, stop=True)
                            last.then_inc(m_ready, 1)
                    if k == 2:
                        pe.wait_ge(wabs_ready, 2)
                        pe.wait_ge(m_copied, H // 4)
                        nc.tensor.matmul(bank_ff[:, 1, 0:2], ones[:, :], wabs[:, :], start=True, stop=True).then_inc(wtot_ready, 1)

            def transpose_ternary(f, k):
                if known(f) and f == 1:
                    pe.wait_ge(wq_ready, 1 if k < 2 else 2)
                    if k:
                        pe.wait_ge(wqT_copied, k)
                    dst = bank_ff[:, 1, :].bitcast(bf16)
                    for j in range(8):
                        if k < 2:
                            src = w1q[:, j * D + k * P:j * D + (k + 1) * P]
                        else:
                            ic, dc = 4 * (k - 2) + j // 2, j % 2
                            src = w2q[:, dc * INNER + ic * P:dc * INNER + (ic + 1) * P]
                        last = nc.tensor.transpose(dst[:, j * P:(j + 1) * P], src, eye_b[:, :])
                    last.then_inc(wqT_ready, 1)

            def scores(f, k, kts):
                n = step_no(f, k)
                lag = 1 if kts == 1 else 0
                if not (known(n) and n <= lag):
                    pe.wait_ge(exp_done, n - lag)
                pe.wait_ge(pair_done, B + n + 1)
                per = GROUP // kts
                b = f // TILES
                for i in range(kts):
                    bank = bank_score[:, k % 2 if kts == 1 else i, :]
                    nc.tensor.matmul(bank.rearrange("p (h s) -> p h s", h=per), eye_b[:, :],
                                     mask[:, bass.ds(f, 1), 0:kts * P].broadcast_to([P, per, kts * P]),
                                     start=True, stop=False, skip_group_check=True)
                    for j in range(per):
                        hh = per * i + j
                        last = nc.tensor.matmul(bank[:, j * kts * P:(j + 1) * kts * P],
                                                qcat[:, k, hh // 2, hh % 2, :], kcat[:, b, hh % 2, 0:kts * P],
                                                start=False, stop=(j == per - 1), skip_group_check=True)
                last.then_inc(score_ready, 1)

            def transpose_probs(f, k, kts):
                n = step_no(f, k)
                pe.wait_ge(exp_done, n + 1)
                for kt in range(kts):
                    if not (known(n) and n * kts + kt == 0):
                        pe.wait_ge(probT_copied, n * kts + kt)
                    for j in range(GROUP):
                        last = nc.tensor.transpose(bank_prob[:, j * P:(j + 1) * P], prob[:, k % 2, j, kt * P:(kt + 1) * P], eye)
                    last.then_inc(probT_ready, 1)

            def values(f, k, kts):
                n = step_no(f, k)
                b = f // TILES
                pe.wait_ge(probT_copied, (n + 1) * kts)
                if not (known(n) and n == 0):
                    pe.wait_ge(latT_copied, n)
                for j in range(GROUP):
                    for kt in range(kts):
                        last = nc.tensor.matmul(bank_lat[:, j * (KVC + 1):(j + 1) * (KVC + 1)], probT[:, k % 2, kt, j, :],
                                                kvc1[:, b * KT + kt, :], start=(kt == 0), stop=(kt == kts - 1))
                last.then_inc(lat_ready, 1)

            def transpose_lat(f, k):
                pe.wait_ge(lat_done, step_no(f, k) + 1)
                for j in range(2):
                    last = nc.tensor.transpose(bank_lat[:, j * P:(j + 1) * P],
                                               lat[:, k % 2, 2 * j:2 * j + 2, :].rearrange("p h c -> p (h c)"), eye)
                last.then_inc(latT_ready, 1)

            def attn_out(c, steps=range(STEPS)):
                pe.wait_ge(latT_copied, c * STEPS + steps[-1] + 1)
                if known(c) and c == 0:
                    pe.wait_ge(m_copied, H // 4)
                elif steps[0] == 0:
                    pe.wait_ge(z_done, 2 * c - 1)
                for j in range(2 * steps[0], 2 * steps[-1] + 2):
                    last = nc.tensor.matmul(bank_ff[:, 0, 0:D], latT[:, j, :], m_sb[:, j, :],
                                            start=(j == 0), stop=(j == PAIRS - 1))
                if steps[-1] == STEPS - 1:
                    last.then_inc(attn_ready, 1)

            def transpose_x(c):
                pe.wait_ge(xq_ready, c + 1)
                if known(c) and c == 0:
                    pe.wait_ge(wqT_copied, 4)
                for j in range(DC):
                    last = nc.tensor.transpose(bank_ff[:, 1, j * P:(j + 1) * P], xl[:, j * P:(j + 1) * P], eye)
                last.then_inc(xqT_ready, 1)

            def up(c, waits=True):
                pe.wait_ge(xqT_copied, c + 1)
                if waits and not (known(c) and c < 2):
                    pe.wait_ge(y_done, c - 1)
                for half in range(2):
                    for j in range(DC):
                        last = nc.tensor.matmul(bank_ff[:, half, :], xqT[:, j, :], w1T[:, j, half * 512:(half + 1) * 512],
                                                start=(j == 0), stop=(j == DC - 1))
                last.then_inc(up_ready, 1)

            def transpose_h(c, r, freed, count):
                if r == 0:
                    pe.wait_ge(hq_ready, c + 1)
                pe.wait_ge(freed, count)
                for j in range(4):
                    last = nc.tensor.transpose(bank_ff[:, 1 - r, j * P:(j + 1) * P],
                                               h[:, slot(c), (4 * r + j) * P:(4 * r + j + 1) * P], eye)
                last.then_inc(hqT_ready, 1)

            def down(c):
                if not last_tile(c):
                    pe.wait_ge(hqT_copied, 2 * c + 2)
                for j in range(IC):
                    if last_tile(c) and j % 4 == 0:
                        pe.wait_ge(hqT_copied, 2 * c + 1 + j // 4)
                    last = nc.tensor.matmul(down_bank(c), hqT[:, j, :], w2T[:, j, :], start=(j == 0), stop=(j == IC - 1))
                last.then_inc(down_ready, 1)

            def feed_forward_mid(f, k):
                if k == 2 and there(f, 3):
                    transpose_h(f - 3, 0, z_done, 2 * (f - 1))
                if k == 3 and there(f, 3):
                    transpose_h(f - 3, 1, x1_done, f)

            def feed_forward_end(f, k):
                if k == 0 and there(f, 2):
                    up(f - 2)
                if k == 1 and there(f, 1):
                    attn_out(f - 1)
                if k == 3 and there(f, 3):
                    down(f - 3)

            def main(kts):
                def body(f):
                    for k in range(STEPS):
                        n = step_no(f, k)
                        if known(n) and n == 0:
                            pe.wait_ge(mask_made, 1)
                        scores(f, k, kts)
                        if not known(f) or n >= 2:
                            transpose_lat(*behind(f, k, 2))
                        if not known(f) or n >= 1:
                            transpose_probs(*behind(f, k, 1), kts)
                        if not known(f) or n + AHEAD < N:
                            project(*ahead(f, k))
                        if k == 0 and there(f, 2):
                            transpose_x(f - 2)
                        feed_forward_mid(f, k)
                        if not known(f) or n >= 1:
                            values(*behind(f, k, 1), kts)
                        feed_forward_end(f, k)
                        prepare_end(f, k)
                        transpose_ternary(f, k)

                def after():
                    transpose_lat(F - 1, STEPS - 2)
                    transpose_x(F - 2)
                    transpose_probs(F - 1, STEPS - 1, kts)
                    up(F - 2)
                    values(F - 1, STEPS - 1, kts)
                    attn_out(F - 1, range(STEPS - 2))
                    transpose_lat(F - 1, STEPS - 1)
                    attn_out(F - 1, range(STEPS - 2, STEPS - 1))
                    attn_out(F - 1, range(STEPS - 1, STEPS))
                    pe.wait_ge(z_done, 2 * (F - 1))
                    transpose_x(F - 1)
                    pe.wait_ge(x1_done, F)
                    up(F - 1, waits=False)
                    transpose_h(F - 3, 0, z_done, 2 * F)
                    transpose_h(F - 3, 1, z_done, 2 * F)
                    down(F - 3)
                    transpose_h(F - 2, 0, hqT_copied, 2 * F - 4)
                    transpose_h(F - 2, 1, y_done, F - 2)
                    down(F - 2)
                    transpose_h(F - 1, 0, hqT_copied, 2 * F - 2)
                    transpose_h(F - 1, 1, y_done, F - 1)
                    down(F - 1)

                run_tiles(pe, body, after)

            choose(pe, main)

        @block.vector
        def _(dve):
            links = {"base": 0, "n": 0}

            def link(ins):
                links["n"] += 1
                ins.then_inc(dve_link, 1)
                dve.wait_ge(dve_link, links["base"] + links["n"])

            nc.vector.memset(ones[:, :], 1.0)
            nc.vector.memset(half_neg[:, :], -0.5)
            nc.vector.memset(eps[:, :], EPS)
            nc.vector.memset(kvc1[:, :, KVC:KVC + 1], 1.0)
            dve.wait_ge(in_sems["eye"], 16)
            nc.vector.tensor_copy(eye_b[:, :], eye).then_inc(consts_made, 1)

            def input_moments(b):
                lo, hi = b * TILES, (b + 1) * TILES
                dve.wait_ge(in_sems[f"x{min(b, 2)}"], 16)
                for f in range(lo, hi):
                    last = nc.vector.bn_stats(a_stats[:, f, :], x_all[:, f, :])
                link(last)
                for f in range(lo, hi):
                    last = nc.vector.bn_aggr(a_mv[:, f, :], a_stats[:, f, :])
                link(last)
                nc.vector.tensor_scalar(a_var[:, lo:hi], a_mv[:, lo:hi, 1], EPS, None, ALU.add).then_inc(a_var_ready, 1)

            def input_norm(b):
                lo, hi = b * TILES, (b + 1) * TILES
                dve.wait_ge(a_root_ready, b + 1)
                for f in range(lo, hi):
                    last = nc.vector.tensor_scalar(xn[:, f, :], x_all[:, f, :], a_mv[:, f, 0:1], a_root[:, f:f + 1],
                                                   ALU.subtract, ALU.mult)
                last.then_inc(xn_ready, 1)

            def copy_ctx(b):
                dve.wait_ge(cT_ready, b + 1)
                if b >= 2:
                    dve.wait_ge(kvc_ready, b - 1)
                nc.vector.tensor_copy(ctxT[:, b % 2, :, :],
                                      input_banks(b)[:, 1, :].rearrange("p (c s) -> p c s", c=DC)).then_inc(cT_copied, 1)

            def turn_keys(b):
                dve.wait_ge(pair_ready, b + 1)
                nc.vector.tensor_tensor(kcat[KVC:P, b, 0, :], bank_pair[KVC:P, 0:S], cos_tab[KVC:P, 0, :], ALU.mult)
                nc.vector.tensor_tensor(kcat[0:R, b, 1, :], bank_pair[0:R, 0:S], cos_tab[0:R, 1, :], ALU.mult)
                if b >= 2:
                    dve.wait_ge(pair_done, b - 1)
                nc.vector.tensor_tensor(turned[:, b % 2, :], bank_swap[:, 0:S], sin_tab, ALU.mult).then_inc(pair_turned, 1)

            input_moments(0)
            input_norm(0)
            copy_ctx(0)
            input_moments(1)

            input_norm(1)
            copy_ctx(1)

            mid = (P - 1) / 2
            dve.wait_ge(in_sems["seg"], 16)
            link(nc.vector.tensor_copy(seg_f[:, :], seg_i[:, :]))
            nc.vector.tensor_scalar(neg_seg[:, :], seg_f[:, :], -1.0, None, ALU.mult).then_inc(seg_ready, 1)
            link(nc.vector.tensor_scalar(far[:, :], seg_f[:, :], mid, None, ALU.subtract))
            link(nc.vector.tensor_tensor(far[:, :], far[:, :], far[:, :], ALU.mult))
            nc.vector.tensor_reduce(farthest[:, 0:1], far[:, :], AX.X, ALU.max).then_inc(far_ready, 1)

            for b in range(2, B):
                input_moments(b)
                if b == 2:
                    dve.wait_ge(in_sems["rope"], 16)
                turn_keys(b - 2)
                input_norm(b)
                copy_ctx(b)
            turn_keys(B - 2)
            turn_keys(B - 1)
            half = R // 2
            for e, o in ((1, 0), (0, KVC)):
                dve.wait_ge(in_sems[f"wqr{e}"], 16)
                nc.vector.tensor_copy(wswap[:, :, o:o + half], wcat[:, :, e, o + half:o + R])
                last = nc.vector.tensor_copy(wswap[:, :, o + half:o + R], wcat[:, :, e, o:o + half])
            last.then_inc(wcopies, 1)
            dve.wait_ge(dist_ready, B)
            for i in range(2):
                last = nc.vector.tensor_scalar(mask[:, i * F // 2:(i + 1) * F // 2, :],
                                               z[:, i, :].rearrange("p (f s) -> p f s", s=S),
                                               (LOOKBACK / 2) ** 2, NEG, ALU.is_gt, ALU.mult)
            last.then_inc(mask_made, 1)

            def copy_fold(i):
                dve.wait_ge(fold_ready, i + 1)
                src = fold_bank(i)[0:QC, 0:4 * KVC].rearrange("k (j e c) -> k j e c", e=2, c=KVC)
                nc.vector.tensor_copy(wcat[:, 2 * i:2 * i + 2, 0, 0:KVC], src[:, :, 0, :])
                nc.vector.tensor_copy(wcat[:, 2 * i:2 * i + 2, 1, R:P], src[:, :, 1, :]).then_inc(fold_copied, 1)

            def turn_step(f, k):
                s = B + step_no(f, k)
                at = (f % TILES) * P
                cos = cos_tab[:, :, bass.ds(at, P)].unsqueeze(1).broadcast_to([P, 2, 2, P])
                sin = sin_tab[:, bass.ds(at, P)].unsqueeze(1).broadcast_to([P, 2, P])
                dve.wait_ge(pair_ready, s + 1)
                if not (known(f) and f == 0):
                    dve.wait_ge(score_ready, step_no(f, k) - STEPS + 1)
                nc.vector.tensor_tensor(qcat[:, k, :, :, :], bank_pair[:, :].rearrange("p (j e s) -> p j e s", j=2, e=2),
                                        cos, ALU.mult)
                dve.wait_ge(pair_done, B if known(f) and step_no(f, k) < 2 else s - 1)
                nc.vector.tensor_tensor(turned[:, k % 2, :].rearrange("p (j s) -> p j s", j=2),
                                        bank_swap[:, 0:S].rearrange("p (j s) -> p j s", j=2), sin, ALU.mult).then_inc(pair_turned, 1)

            copy_fold(0)
            copy_fold(1)
            turn_step(0, 0)
            copy_fold(2)
            copy_fold(3)
            dve.wait_ge(far_turned, 1)
            link(nc.vector.tensor_reduce(farthest[0:1, 1:2], bank_ff[0:1, 0, 0:P], AX.X, ALU.max))
            nc.vector.tensor_scalar(wide[:, :], farthest[0:1, 1:2], mid * mid, None, ALU.is_gt).then_inc(wide_ready, 1)
            turn_step(0, 1)

            def prepare(f, k):
                if not known(f):
                    return
                if f == 0 and k in (1, 2):
                    for i in (2 * k - 2, 2 * k - 1):
                        dve.wait_ge(m_ready, i + 1)
                        nc.vector.tensor_copy(m_sb[:, 2 * i:2 * i + 2, :],
                                              bank_ff[:, i % 2, :].rearrange("p (j n) -> p j n", j=2)).then_inc(m_copied, 1)
                if f == 0 and k == 2:
                    dve.wait_ge(wtot_ready, 1)
                    link(nc.vector.tensor_scalar(wmean[:, :], bank_ff[:, 1, 0:2], 1.0 / (INNER * D), 1e-5, ALU.mult, ALU.max))
                    link(nc.vector.reciprocal(winv[:, :], wmean[:, :]))
                for i, part in {(0, 2): ((0, 0),), (0, 3): ((0, 1), (0, 2)), (1, 0): ((1, 0),),
                                (1, 1): ((1, 1), (1, 2))}.get((f, k), ()):
                    ternary(i, part)

            def ternary(i, part):
                src, dst = ((w1_sb, w1q), (w2_sb, w2q))[i]
                src = src[:, :, :].rearrange("p c n -> p (c n)")
                if part == 0:
                    link(nc.vector.tensor_scalar(src, src, winv[:, i:i + 1], 1.0, ALU.mult, ALU.min))
                elif part == 1:
                    link(nc.vector.tensor_scalar(src, src, -1.0, MAGIC, ALU.max, ALU.add))
                else:
                    nc.vector.tensor_scalar(dst[:, :], src, MAGIC, None, ALU.subtract).then_inc(wq_ready, 1)

            def absmax(src, small):
                links["n"] += 1
                nc.vector.tensor_reduce(small(AMAX), src, AX.X, ALU.max, apply_absolute_value=True).then_inc(dve_link, 1)
                return links["n"]

            def quantise(src, small, layer, amax, root, count, deq, ready):
                dve.wait_ge(root, count)
                dve.wait_ge(dve_link, links["base"] + amax)
                link(nc.vector.tensor_scalar(small(YMAX), small(AMAX), small(RRMS), 1e-5, ALU.mult, ALU.max))
                nc.vector.tensor_scalar(deq, small(YMAX), 1.0 / QMAX, wmean[:, layer:layer + 1], ALU.mult, ALU.mult)
                link(nc.vector.reciprocal(small(YINV), small(YMAX)))
                link(nc.vector.tensor_scalar(small(QMUL), small(YINV), QMAX, small(RRMS), ALU.mult, ALU.mult))
                nc.vector.tensor_scalar(src, src, small(QMUL), MAGIC, ALU.mult, ALU.add).then_inc(ready, 1)

            def take_wait(i=0):
                nc.vector.memset(pad[:, i:i + 1], 0.0)

            def first_product(c):
                dve.wait_ge(up_ready, c + 1)
                for i, part in enumerate(halves):
                    nc.vector.scalar_tensor_tensor(z[:, slot(c), part], bank_ff[:, i, :], x_deq[:, 0:1], b1_bc[:, part],
                                                   ALU.mult, ALU.add).then_inc(z_done, 1)

            def silu(c):
                for i, part in enumerate(halves):
                    dve.wait_ge(tanh_done, 2 * c + i + 1)
                    nc.vector.scalar_tensor_tensor(z[:, slot(c), part], tanh_z[:, part], 1.0, z[:, slot(c), part],
                                                   ALU.add, ALU.mult).then_inc(silu_done, 1)

            def moments_h(c):
                for i, part in enumerate(halves):
                    dve.wait_ge(gelu_done, 2 * c + i + 1)
                    take_wait(i)
                    last = nc.vector.bn_stats(h_stats[:, 6 * i:6 * i + 6], z[:, slot(c), part])
                link(last)
                take_wait()
                nc.vector.bn_aggr(h_mv[:, :], h_stats[:, :]).then_inc(h_moments, 1)

            def layer_norm_h(c):
                dst = h[:, slot(c), :]
                dve.wait_ge(h_rstd, c + 1)
                link(nc.vector.scalar_tensor_tensor(dst, z[:, slot(c), :], h_mv[:, 0:1], g_bc[:, :], ALU.subtract, ALU.mult))
                nc.vector.scalar_tensor_tensor(dst, dst, hs(RSTD), lb_bc[:, :], ALU.mult, ALU.add).then_inc(h_ready, 1)

            def quantise_h(c, between=None):
                dve.wait_ge(h_ready, c + 1)
                amax = absmax(h[:, slot(c), :], hs)
                if between:
                    between()
                quantise(h[:, slot(c), :], hs, 1, amax, h_rrms, c + 1, h_deq[:, 0:1], hq_ready)

            def residual_and_quantise(c):
                x1 = x_all[:, c, :]
                dve.wait_ge(attn_ready, c + 1)
                nc.vector.scalar_tensor_tensor(x1, bank_ff[:, 0, 0:D], tgate[:, 0:1], x1, ALU.mult, ALU.add).then_inc(x1_done, 1)
                dve.wait_ge(x1_done, c + 1)
                take_wait()
                link(nc.vector.bn_stats(x_stats[:, :], x1))
                take_wait()
                link(nc.vector.bn_aggr(x_mv[:, :], x_stats[:, :]))
                link(nc.vector.tensor_scalar(xs(VAR), x_mv[:, 1:2], EPS, EPS, ALU.add, ALU.mult))
                nc.vector.tensor_tensor(xs(MS), xs(VAR), x_mv[:, 1:2], ALU.add).then_inc(x_moments, 1)
                link(nc.vector.tensor_scalar(xl[:, :], x1, x_mv[:, 0:1], None, ALU.subtract))
                quantise(xl[:, :], xs, 0, absmax(xl[:, :], xs), x_root, c + 1, x_deq[:, 0:1], xq_ready)

            def output(c):
                dve.wait_ge(down_ready, c + 1)
                link(nc.vector.scalar_tensor_tensor(ytmp[:, :], down_bank(c), h_deq[:, 0:1], b2_bc[:, :],
                                                    ALU.mult, ALU.add))
                if not (known(c) and c == 0):
                    dve.wait_ge(out_stored, 16 * c)
                nc.vector.scalar_tensor_tensor(y[:, :], ytmp[:, :], tgate[:, 1:2], x_all[:, c, :],
                                               ALU.mult, ALU.add).then_inc(y_done, 1)

            def feed_forward(f, k):
                if k == 0 and there(f, 3):
                    layer_norm_h(f - 3)
                if k == 1 and there(f, 3):
                    quantise_h(f - 3, lambda: silu(f - 2))
                elif k == 1 and there(f, 2):
                    silu(f - 2)
                if k == 2 and there(f, 1):
                    residual_and_quantise(f - 1)
                if k == 3:
                    stages = [(moments_h, 2), (output, 3)]
                    if known(f) and f == F - 1:
                        stages.reverse()
                    for stage, lag in stages:
                        if there(f, lag):
                            stage(f - lag)

            def softmax_max(f, k, kts):
                n = step_no(f, k)
                dve.wait_ge(score_ready, n + 1)
                if not (known(n) and n < 2):
                    dve.wait_ge(exp_done, n - 1)
                nc.vector.tensor_reduce(neg_max[:, k % 2, :], score_banks(k, kts), AX.X, ALU.max,
                                        negate=True).then_inc(max_done, 1)

            def normalise(f, k):
                n = step_no(f, k)
                dve.wait_ge(lat_ready, n + 1)
                src = bank_lat[:, 0:GROUP * (KVC + 1)].rearrange("p (h c) -> p h c", h=GROUP)
                nc.vector.reciprocal(rsum[:, k % 2, :], src[:, :, KVC]).then_inc(rsum_done, 1)
                if not (known(n) and n < 2):
                    dve.wait_ge(latT_ready, n - 1)
                dve.wait_ge(rsum_done, n + 1)
                nc.vector.tensor_tensor(lat[:, k % 2, :, :], src[:, :, 0:KVC],
                                        rsum[:, k % 2, :].unsqueeze(2).broadcast_to([P, GROUP, KVC]),
                                        ALU.mult).then_inc(lat_done, 1)

            dve.wait_ge(gates_done, 1)
            for name in ("b1", "b2", "g", "lb"):
                dve.wait_ge(in_sems[name], 16)
            LINKS = 15
            so_far = links["n"]

            def main(kts):
                links["base"], links["n"] = so_far, 0

                def before(f):
                    if f is None:
                        links["start"] = links["base"] + links["n"]
                    elif not known(f):
                        links["base"], links["n"] = links["start"] + (f - LEAD) * LINKS, 0
                    elif f == F - 1:
                        links["base"], links["n"] = links["start"] + (F - 1 - LEAD) * LINKS, 0

                def body(f):
                    for k in range(STEPS):
                        n = step_no(f, k)
                        if k == 1 and there(f, 2):
                            first_product(f - 2)
                        softmax_max(f, k, kts)
                        if not known(f) or n + AHEAD < N:
                            turn_step(*ahead(f, k))
                        if not known(f) or n >= 1:
                            normalise(*behind(f, k, 1))
                        prepare(f, k)
                        feed_forward(f, k)
                    assert known(f) or links["n"] == LINKS, links["n"]

                def after():
                    first_product(F - 2)
                    normalise(F - 1, STEPS - 1)
                    layer_norm_h(F - 3)
                    residual_and_quantise(F - 1)
                    moments_h(F - 2)
                    quantise_h(F - 3, lambda: first_product(F - 1))
                    layer_norm_h(F - 2)
                    quantise_h(F - 2, lambda: (moments_h(F - 1), output(F - 3)))
                    layer_norm_h(F - 1)
                    quantise_h(F - 1, lambda: output(F - 2))
                    output(F - 1)

                run_tiles(dve, body, after, before)

            choose(dve, main)


_INS = ['x', 'ctx_2048', 'itok_BxS_0_1023', 'g_xattn', 'g_ffn', 'L0_xattn_W_kvc', 'L0_xattn_W_dq',
        'L0_xattn_W_uq', 'L0_xattn_W_qr', 'L0_xattn_W_uk', 'L0_xattn_W_kr', 'L0_xattn_W_uv', 'L0_xattn_W_o',
        'L0_ffn_w1', 'L0_ffn_b1', 'L0_ffn_ln_g', 'L0_ffn_ln_b', 'L0_ffn_w2', 'L0_ffn_b2']


def kernel(**inputs):
    import numpy as _np
    import concourse.bacc as _bacc
    from concourse import mybir as _mybir
    from concourse.bass_utils import run_bass_kernel_spmd as _run

    nc = _bacc.Bacc("TRN2", target_bir_lowering=False, num_devices=1)
    arrays, args = {}, []
    for name in _INS:
        a = _np.ascontiguousarray(inputs[name])
        arrays[f"in_{name}"] = a
        args.append(nc.dram_tensor(f"in_{name}", a.shape, _mybir.dt.from_np(a.dtype), kind="ExternalInput").ap())
    c = shape_constants()
    arrays["in_consts"] = c
    args.append(nc.dram_tensor("in_consts", c.shape, _mybir.dt.from_np(c.dtype), kind="ExternalInput").ap())
    args.append(nc.dram_tensor("out_x", (B, S, D), _mybir.dt.float32, kind="ExternalOutput").ap())
    build(nc, *args)
    r = _run(nc, [arrays], core_ids=[0])
    return r.results[0]["out_x"]
```
